# Optimizing a Trainium2 kernel written in Bass

```python
import numpy as np
import jax
import jax.numpy as jnp

def _softmax(x, axis=-1):
    return jax.nn.softmax(x, axis=axis)

def _gelu(x):
    return jax.nn.gelu(x, approximate=True)

def _silu(x):
    return jax.nn.silu(x)

def _sigmoid(x):
    return jax.nn.sigmoid(x)

def _layernorm(x, axis=-1, eps=1e-05):
    m = jnp.mean(x, axis=axis, keepdims=True)
    v = jnp.var(x, axis=axis, keepdims=True)
    return (x - m) / jnp.sqrt(v + eps)

def _scatter_add(tgt, idx, src, axis=0):
    return tgt.at[idx].add(src)

def _segment_sum(src, seg, n):
    return jax.ops.segment_sum(src, seg, n)
kernel_name = 'mk_adaln_d2_jaxref_r8_11cbec'

def setup_inputs(seed: int=0):
    np.random.seed(seed)
    _w = jnp.asarray

    def _L0_attn_setup():
        import jax, jax.numpy as jnp
        import numpy as np
        B, S, DM, H, DH = (2, 256, 128, 16, 64)
        HID = H * DH

        def _xavier(key, shape):
            fan_out, fan_in = shape
            lim = float(np.sqrt(6.0 / (fan_in + fan_out)))
            return jax.random.uniform(key, shape, jnp.float32, -lim, lim)

        def _gla_scan(q, k, v, g):
            qt = jnp.moveaxis(q, 1, 0)
            kt = jnp.moveaxis(k, 1, 0)
            vt = jnp.moveaxis(v, 1, 0)
            gt = jnp.moveaxis(g, 1, 0)

            def step(s, inp):
                qi, ki, vi, gi = inp
                s = jnp.exp(gi)[:, :, None, None] * s + ki[..., :, None] * vi[..., None, :]
                o = jnp.einsum('bhk,bhkv->bhv', qi, s)
                return (s, o)
            s0 = jnp.zeros(q.shape[0:1] + q.shape[2:] + q.shape[-1:], q.dtype)
            _, o = jax.lax.scan(step, s0, (qt, kt, vt, gt))
            return jnp.moveaxis(o, 0, 1)
        key = jax.random.key(seed)
        ks = jax.random.split(key, 8)
        return {'x': jax.random.normal(ks[0], (B, S, DM), jnp.float32), 'Wq': _xavier(ks[1], (HID, DM)), 'Wk': _xavier(ks[2], (HID, DM)), 'Wv': _xavier(ks[3], (HID, DM)), 'Wo': _xavier(ks[4], (DM, HID)), 'Wg': _xavier(ks[5], (HID, DM)), 'Wog': _xavier(ks[6], (HID, DM)), 'Wd': _xavier(ks[7], (H, DM)), 'bd': jnp.full((H,), -2.0, jnp.float32), 'norm_w': jnp.ones((HID,), jnp.float32)}
    _L0_attn_in = _L0_attn_setup()

    def _L0_ffn_setup():
        import jax, jax.numpy as jnp
        import numpy as np
        B, S, D = (2, 64, 128)
        E, K, I = (16, 8, 128)
        I_SH = 128
        ROUTE_SCALE = 2.826
        key = jax.random.key(seed)
        ks = jax.random.split(key, 8)
        s = 0.02
        return {'x': jax.random.normal(ks[0], (B, S, D), dtype=jnp.float32), 'gate_w': jax.random.normal(ks[1], (E, D), dtype=jnp.float32) * s, 'expert_bias': jnp.zeros((E,), dtype=jnp.float32), 'w_gate': jax.random.normal(ks[2], (E, I, D), dtype=jnp.float32) * s, 'w_up': jax.random.normal(ks[3], (E, I, D), dtype=jnp.float32) * s, 'w_down': jax.random.normal(ks[4], (E, D, I), dtype=jnp.float32) * s, 'shared_gate_w': jax.random.normal(ks[5], (I_SH, D), dtype=jnp.float32) * s, 'shared_up_w': jax.random.normal(ks[6], (I_SH, D), dtype=jnp.float32) * s, 'shared_down_w': jax.random.normal(ks[7], (D, I_SH), dtype=jnp.float32) * s}
    _L0_ffn_in = _L0_ffn_setup()
    _L0_c = _w((lambda *s: np.random.randn(*s).astype(np.float32) * 0.05)(8, 128))
    _L0_wmod = _w((lambda *s: np.random.randn(*s).astype(np.float32) * 0.05)(128, 6 * 128) * 128 ** (-0.5))

    def _L1_attn_setup():
        import jax, jax.numpy as jnp
        import numpy as np
        B, N, QD = (4, 512, 128)
        HEADS, DIM_HEAD = (8, 64)
        HID = HEADS * DIM_HEAD
        SCALE = DIM_HEAD ** (-0.5)
        key = jax.random.key(seed)
        ks = jax.random.split(key, 6)
        s_in = 1.0 / np.sqrt(QD)
        s_h = 1.0 / np.sqrt(HID)
        return {'x': jax.random.normal(ks[0], (B, N, QD), dtype=jnp.float32), 'Wq': jax.random.uniform(ks[1], (QD, HID), jnp.float32, -s_in, s_in), 'Wk': jax.random.uniform(ks[2], (QD, HID), jnp.float32, -s_in, s_in), 'Wv': jax.random.uniform(ks[3], (QD, HID), jnp.float32, -s_in, s_in), 'Wo': jax.random.uniform(ks[4], (HID, QD), jnp.float32, -s_h, s_h), 'bo': jax.random.uniform(ks[5], (QD,), jnp.float32, -s_h, s_h)}
    _L1_attn_in = _L1_attn_setup()

    def _L1_ffn_setup():
        import jax, jax.numpy as jnp
        import numpy as np
        N_EMBD = 128
        NUM_EXPERTS = 8
        TOP_K = 2
        D_FF = 4 * N_EMBD
        B, S = (4, 256)
        key = jax.random.key(seed)
        ks = jax.random.split(key, 7)
        scale = lambda fan_in: 1.0 / np.sqrt(fan_in)
        x = jax.random.normal(ks[0], (B, S, N_EMBD), dtype=jnp.float32)
        W_router = jax.random.normal(ks[1], (N_EMBD, NUM_EXPERTS), dtype=jnp.float32) * scale(N_EMBD)
        b_router = jnp.zeros((NUM_EXPERTS,), dtype=jnp.float32)
        W1 = jax.random.normal(ks[2], (NUM_EXPERTS, N_EMBD, D_FF), dtype=jnp.float32) * scale(N_EMBD)
        b1 = jnp.zeros((NUM_EXPERTS, D_FF), dtype=jnp.float32)
        W2 = jax.random.normal(ks[3], (NUM_EXPERTS, D_FF, N_EMBD), dtype=jnp.float32) * scale(D_FF)
        b2 = jnpp = jnp.zeros((NUM_EXPERTS, N_EMBD), dtype=jnp.float32)
        return {'x': x, 'W_router': W_router, 'b_router': b_router, 'W1': W1, 'b1': b1, 'W2': W2, 'b2': b2}
    _L1_ffn_in = _L1_ffn_setup()
    _L1_c = _w((lambda *s: np.random.randn(*s).astype(np.float32) * 0.05)(8, 128))
    _L1_wmod = _w((lambda *s: np.random.randn(*s).astype(np.float32) * 0.05)(128, 6 * 128) * 128 ** (-0.5))
    _d = {'L0_attn_x': _L0_attn_in['x'], 'L0_attn_Wq': _L0_attn_in['Wq'], 'L0_attn_Wk': _L0_attn_in['Wk'], 'L0_attn_Wv': _L0_attn_in['Wv'], 'L0_attn_Wo': _L0_attn_in['Wo'], 'L0_attn_Wg': _L0_attn_in['Wg'], 'L0_attn_Wog': _L0_attn_in['Wog'], 'L0_attn_Wd': _L0_attn_in['Wd'], 'L0_attn_bd': _L0_attn_in['bd'], 'L0_attn_norm_w': _L0_attn_in['norm_w'], 'L0_ffn_gate_w': _L0_ffn_in['gate_w'], 'L0_ffn_expert_bias': _L0_ffn_in['expert_bias'], 'L0_ffn_w_gate': _L0_ffn_in['w_gate'], 'L0_ffn_w_up': _L0_ffn_in['w_up'], 'L0_ffn_w_down': _L0_ffn_in['w_down'], 'L0_ffn_shared_gate_w': _L0_ffn_in['shared_gate_w'], 'L0_ffn_shared_up_w': _L0_ffn_in['shared_up_w'], 'L0_ffn_shared_down_w': _L0_ffn_in['shared_down_w'], 'L0_c': _L0_c, 'L0_wmod': _L0_wmod, 'L1_attn_Wq': _L1_attn_in['Wq'], 'L1_attn_Wk': _L1_attn_in['Wk'], 'L1_attn_Wv': _L1_attn_in['Wv'], 'L1_attn_Wo': _L1_attn_in['Wo'], 'L1_attn_bo': _L1_attn_in['bo'], 'L1_ffn_W_router': _L1_ffn_in['W_router'], 'L1_ffn_b_router': _L1_ffn_in['b_router'], 'L1_ffn_W1': _L1_ffn_in['W1'], 'L1_ffn_b1': _L1_ffn_in['b1'], 'L1_ffn_W2': _L1_ffn_in['W2'], 'L1_ffn_b2': _L1_ffn_in['b2'], 'L1_c': _L1_c, 'L1_wmod': _L1_wmod}
    _x0 = _d['L0_attn_x']
    _d['L0_attn_x'] = jax.random.normal(jax.random.fold_in(jax.random.key(seed), 1), (8, 256, 128), dtype=_x0.dtype)
    del _x0
    return _d

def reference(L0_attn_x, L0_attn_Wq, L0_attn_Wk, L0_attn_Wv, L0_attn_Wo, L0_attn_Wg, L0_attn_Wog, L0_attn_Wd, L0_attn_bd, L0_attn_norm_w, L0_ffn_gate_w, L0_ffn_expert_bias, L0_ffn_w_gate, L0_ffn_w_up, L0_ffn_w_down, L0_ffn_shared_gate_w, L0_ffn_shared_up_w, L0_ffn_shared_down_w, L0_c, L0_wmod, L1_attn_Wq, L1_attn_Wk, L1_attn_Wv, L1_attn_Wo, L1_attn_bo, L1_ffn_W_router, L1_ffn_b_router, L1_ffn_W1, L1_ffn_b1, L1_ffn_W2, L1_ffn_b2, L1_c, L1_wmod):

    def _L0_attn_ref(x, Wq, Wk, Wv, Wo, Wg, Wog, Wd, bd, norm_w):
        import jax, jax.numpy as jnp
        import numpy as np
        B, S, DM, H, DH = (2, 256, 128, 16, 64)
        HID = H * DH

        def _xavier(key, shape):
            fan_out, fan_in = shape
            lim = float(np.sqrt(6.0 / (fan_in + fan_out)))
            return jax.random.uniform(key, shape, jnp.float32, -lim, lim)

        def _gla_scan(q, k, v, g):
            qt = jnp.moveaxis(q, 1, 0)
            kt = jnp.moveaxis(k, 1, 0)
            vt = jnp.moveaxis(v, 1, 0)
            gt = jnp.moveaxis(g, 1, 0)

            def step(s, inp):
                qi, ki, vi, gi = inp
                s = jnp.exp(gi)[:, :, None, None] * s + ki[..., :, None] * vi[..., None, :]
                o = jnp.einsum('bhk,bhkv->bhv', qi, s)
                return (s, o)
            s0 = jnp.zeros(q.shape[0:1] + q.shape[2:] + q.shape[-1:], q.dtype)
            _, o = jax.lax.scan(step, s0, (qt, kt, vt, gt))
            return jnp.moveaxis(o, 0, 1)
        b, s, _ = x.shape
        q = (x @ Wq.T).reshape(b, s, H, DH)
        k = (x @ Wk.T).reshape(b, s, H, DH)
        v = (x @ Wv.T).reshape(b, s, H, DH)
        log_decay = -jax.nn.softplus(x @ Wd.T + bd)
        gate = jax.nn.sigmoid((x @ Wg.T).reshape(b, s, H, DH))
        k_gated = k * gate
        out = _gla_scan(q, k_gated, v, log_decay)
        out = out.reshape(b, s, HID)
        eps = jnp.finfo(out.dtype).eps
        out = out * jax.lax.rsqrt(jnp.mean(out * out, -1, keepdims=True) + eps) * norm_w
        out = out * jax.nn.sigmoid(x @ Wog.T)
        return out @ Wo.T

    def _L0_ffn_ref(x, gate_w, expert_bias, w_gate, w_up, w_down, shared_gate_w, shared_up_w, shared_down_w):
        import jax, jax.numpy as jnp
        import numpy as np
        B, S, D = (2, 64, 128)
        E, K, I = (16, 8, 128)
        I_SH = 128
        ROUTE_SCALE = 2.826
        gates = jnp.einsum('bsd,ed->bse', x, gate_w)
        scores = jax.nn.sigmoid(gates.astype(jnp.float32))
        sel_scores = scores + expert_bias
        _, inds = jax.lax.top_k(sel_scores, K)
        selected = jnp.take_along_axis(scores, inds, axis=-1)
        selected = selected / selected.sum(axis=-1, keepdims=True)
        selected = selected * ROUTE_SCALE
        onehot = jax.nn.one_hot(inds, E, dtype=selected.dtype)
        combine = jnp.einsum('bske,bsk->bse', onehot, selected)
        hg = jnp.einsum('bsd,eid->bsei', x, w_gate)
        hu = jnp.einsum('bsd,eid->bsei', x, w_up)
        h = jax.nn.silu(hg) * hu
        ye = jnp.einsum('bsei,edi->bsed', h, w_down)
        y = jnp.einsum('bsed,bse->bsd', ye, combine).astype(x.dtype)
        g = jnp.einsum('bsd,id->bsi', x, shared_gate_w)
        u = jnp.einsum('bsd,id->bsi', x, shared_up_w)
        y = y + jnp.einsum('bsi,di->bsd', jax.nn.silu(g) * u, shared_down_w)
        return y

    def _L1_attn_ref(x, Wq, Wk, Wv, Wo, bo):
        import jax, jax.numpy as jnp
        import numpy as np
        B, N, QD = (4, 512, 128)
        HEADS, DIM_HEAD = (8, 64)
        HID = HEADS * DIM_HEAD
        SCALE = DIM_HEAD ** (-0.5)
        b, n, _ = x.shape
        q = x @ Wq
        k = x @ Wk
        v = x @ Wv

        def split_heads(t):
            return t.reshape(b, n, HEADS, DIM_HEAD).transpose(0, 2, 3, 1)
        q = split_heads(q)
        k = split_heads(k)
        v = split_heads(v)
        q = jax.nn.softmax(q, axis=-2) * SCALE
        k = jax.nn.softmax(k, axis=-1)
        context = jnp.einsum('bhdn,bhen->bhde', k, v)
        out = jnp.einsum('bhde,bhdn->bhen', context, q)
        out = out.transpose(0, 3, 1, 2).reshape(b, n, HID)
        return out @ Wo + bo

    def _L1_ffn_ref(x, W_router, b_router, W1, b1, W2, b2):
        import jax, jax.numpy as jnp
        import numpy as np
        N_EMBD = 128
        NUM_EXPERTS = 8
        TOP_K = 2
        D_FF = 4 * N_EMBD
        B, S = (4, 256)
        Bv, Sv, D = x.shape
        flat_x = x.reshape(-1, D)
        T = flat_x.shape[0]
        logits = flat_x @ W_router + b_router
        top_vals, top_idx = jax.lax.top_k(logits, TOP_K)
        neg_inf = jnp.full_like(logits, -jnp.inf)
        sparse_logits = neg_inf.at[jnp.arange(T)[:, None], top_idx].set(top_vals)
        router_weights = jax.nn.softmax(sparse_logits, axis=-1)
        final_output = jnp.zeros_like(flat_x)
        for e in range(NUM_EXPERTS):
            expert_mask = jnp.any(top_idx == e, axis=-1)
            h = jax.nn.relu(flat_x @ W1[e] + b1[e])
            y = h @ W2[e] + b2[e]
            w = router_weights[:, e] * expert_mask.astype(x.dtype)
            final_output = final_output + y * w[:, None]
        return final_output.reshape(Bv, Sv, D)
    x = L0_attn_x
    mod = (_silu(L0_c) @ L0_wmod).reshape(L0_c.shape[0], 6, 1, -1)
    sa, ca, ga, sb, cb, gb = (mod[:, 0], mod[:, 1], mod[:, 2], mod[:, 3], mod[:, 4], mod[:, 5])
    ga = (2 * (ga >= 0) - 1) * jnp.maximum(jnp.abs(ga), 0.25)
    gb = (2 * (gb >= 0) - 1) * jnp.maximum(jnp.abs(gb), 0.25)
    h = _layernorm(x, axis=-1) * (1 + ca) + sa
    x = x + ga * _L0_attn_ref(h, L0_attn_Wq, L0_attn_Wk, L0_attn_Wv, L0_attn_Wo, L0_attn_Wg, L0_attn_Wog, L0_attn_Wd, L0_attn_bd, L0_attn_norm_w)
    h = _layernorm(x, axis=-1) * (1 + cb) + sb
    x = x + gb * _L0_ffn_ref(h, L0_ffn_gate_w, L0_ffn_expert_bias, L0_ffn_w_gate, L0_ffn_w_up, L0_ffn_w_down, L0_ffn_shared_gate_w, L0_ffn_shared_up_w, L0_ffn_shared_down_w)
    mod = (_silu(L1_c) @ L1_wmod).reshape(L1_c.shape[0], 6, 1, -1)
    sa, ca, ga, sb, cb, gb = (mod[:, 0], mod[:, 1], mod[:, 2], mod[:, 3], mod[:, 4], mod[:, 5])
    ga = (2 * (ga >= 0) - 1) * jnp.maximum(jnp.abs(ga), 0.25)
    gb = (2 * (gb >= 0) - 1) * jnp.maximum(jnp.abs(gb), 0.25)
    h = _layernorm(x, axis=-1) * (1 + ca) + sa
    x = x + ga * _L1_attn_ref(h, L1_attn_Wq, L1_attn_Wk, L1_attn_Wv, L1_attn_Wo, L1_attn_bo)
    h = _layernorm(x, axis=-1) * (1 + cb) + sb
    x = x + gb * _L1_ffn_ref(h, L1_ffn_W_router, L1_ffn_b_router, L1_ffn_W1, L1_ffn_b1, L1_ffn_W2, L1_ffn_b2)
    return x

_drawn_inputs = setup_inputs


def setup_inputs(seed=0):
    import zlib

    import numpy as np

    out = dict(_drawn_inputs(seed))
    spreads = {'L0_attn_bd': (-2.0, 0.2),
     'L0_attn_norm_w': (1.0, 0.2),
     'L0_ffn_expert_bias': (0.0, 0.8),
     'L1_ffn_b_router': (0.0, 0.33),
     'L1_ffn_b1': (0.0, 0.616),
     'L1_ffn_b2': (0.0, 0.43)}
    factors = {'L0_ffn_gate_w': 8.0,
     'L0_ffn_w_gate': 8.0,
     'L0_ffn_w_up': 8.0,
     'L0_ffn_w_down': 8.0,
     'L0_ffn_shared_gate_w': 8.0,
     'L0_ffn_shared_up_w': 8.0,
     'L0_ffn_shared_down_w': 8.0,
     'L1_attn_Wq': 8.0,
     'L1_attn_Wk': 8.0,
     'L1_attn_Wv': 8.0,
     'L1_attn_Wo': 8.0,
     'L1_attn_bo': 5.76}
    for name, (base, spread) in spreads.items():
        noise = np.random.default_rng([zlib.crc32(name.encode()), seed]).standard_normal(out[name].shape)
        drawn = base * np.exp(spread * noise) if base else spread * noise
        out[name] = jnp.asarray(drawn.astype(out[name].dtype))
    for name, factor in factors.items():
        out[name] = (out[name] * factor).astype(out[name].dtype)
    return out
```

```python
from contextlib import ExitStack

import numpy as np

import concourse.bass as bass
from concourse import mybir
from concourse.alu_op_type import AluOpType as ALU

ACT = mybir.ActivationFunctionType
AX_X = mybir.AxisListType.X
F32 = mybir.dt.float32
F32R = mybir.dt.float32r

P = 128
D = 128
B = 8
S = 256
TT = S // P
NT = B * TT
NG = 4
GT = NT // NG
GW = GT * P

H0, DH = 16, 64
HID0 = H0 * DH
HT0 = HID0 // P
HALF = H0 // 2
E0 = 16
K0 = 8
ROUTE_SCALE = 2.826
H1 = 8
HID1 = H1 * DH
HT1 = HID1 // P
E1 = 8
FT = 4
LN_EPS = 1e-5
RMS_EPS = float(np.finfo(np.float32).eps)
BIG = 3.0e38

MISC = {}
_at = 0
for _name, _n in (("c", 2 * B), ("wd", H0), ("bd", H0), ("norm_w", HT0), ("gate_w", E0), ("ebias", E0),
                  ("w_router", E1), ("b_router", E1), ("bo", D)):
    MISC[_name] = (_at, _at + _n)
    _at += _n
MISC_W = _at


class Banks:

    def __init__(self):
        self.base = [0] * 8

    def phase(self, table, times=1):
        u = Uses(list(self.base), table)
        for k in range(8):
            self.base[k] += u.per[k] * times
        return u


class Uses:
    def __init__(self, base, table):
        self.at, self.base, self.per = {}, base, [0] * 8
        self.marks = {}
        for name, bank in table:
            if bank is None:
                self.marks[name] = list(self.per)
                continue
            self.at[name] = (bank, self.per[bank])
            self.per[bank] += 1

    def before(self, mark, bank, i=0):
        return self.per[bank] * i + (self.base[bank] + self.marks[mark][bank])

    def bank(self, name):
        return self.at[name][0]

    def free(self, name, i=0):
        bank, n = self.at[name]
        return self.per[bank] * i + (self.base[bank] + n)

    def done(self, name, i=0):
        bank, n = self.at[name]
        return self.per[bank] * i + (self.base[bank] + n + 1)


class Chain:

    def __init__(self, sem):
        self.sem, self.base, self.k, self.i, self.per = sem, 0, 0, 0, 0

    def loop(self, i, per):
        self.base, self.k, self.i, self.per = self.base + self.k, 0, i, per

    def end(self, times):
        assert self.k == self.per, (self.k, self.per)
        self.base, self.k, self.i, self.per = self.base + self.per * times, 0, 0, 0

    def __call__(self, eng, ins):
        ins.then_inc(self.sem, 1)
        self.k += 1
        eng.wait_ge(self.sem, self.per * self.i + (self.base + self.k))


def build(nc, x, misc, wmod, wa, woT, w_ffn0, w_l1, wo1, w_ffn1, b2, out, phases=4):
    gate_scratch = nc.dram_tensor("gate_scratch", (2, 2, B, D), F32).ap()
    decay_scratch = nc.dram_tensor("decay_scratch", (2, H0, NT * P), F32).ap()
    x_tiles = x.rearrange("b (h p) d -> p (b h) d", p=P)
    out_tiles = out.rearrange("b (h p) d -> p (b h) d", p=P)

    banks = Banks()

    ctx = ExitStack()
    with ctx:
        def sb(name, shape, dt=F32, stack=ctx):
            return stack.enter_context(nc.sbuf_tensor(name, shape, dt))

        def sem(name):
            return ctx.enter_context(nc.semaphore(name))

        bank = [ctx.enter_context(nc.psum_tensor(f"bank{k}", [P, 512], F32)) for k in range(8)]
        filled = [sem(f"filled{k}") for k in range(8)]
        emptied = [sem(f"emptied{k}") for k in range(8)]

        X = sb("X", [P, NT, D])
        HT = sb("HT", [P, 2, NT * P], F32R)
        HTB = sb("HTB", [P, 2, 2, S], F32R)
        GB = sb("GB", [P, 2, B, D])
        MODT = sb("MODT", [P, 2, 4, B])
        M = sb("M", [P, MISC_W])
        IDN = sb("IDN", [P, P])
        XH = sb("XH", [P, 2, GT, D])
        H32 = sb("H32", [P, 2, GW])
        ST = sb("ST", [P, NT, 6])
        MV = sb("MV", [P, NT, 2])
        RS = sb("RS", [P, NT])
        SC = sb("SC", [P, 2, B])
        MHALF = sb("MHALF", [P, GT])
        COMB = sb("COMB", [P, NT, E0 + 1])
        B2 = sb("B2", [E1, D])
        FW = sb("FW", [P, 2, 3, P])
        FWH = sb("FWH", [P, 2, 2 * P], F32R)
        FWL = sb("FWL", [P, 2, 2 * P], F32R)

        def misc_of(name):
            a, b = MISC[name]
            return M[:, a:b]

        s_misc = sem("s_misc")
        s_mod = sem("s_mod")
        s_x = [sem(f"s_x{g}") for g in range(NG)]
        s_silu = sem("s_silu")
        s_idn = sem("s_idn")
        s_tri = sem("s_tri")
        s_rows_in = sem("s_rows_in")
        s_rows = sem("s_rows")
        s_gates = sem("s_gates")
        s_gates_out = sem("s_gates_out")
        s_gb = sem("s_gb")
        s_wa_raw = [sem(f"s_wa_raw{k}") for k in range(2)]
        s_wa_hi = sem("s_wa_hi")
        s_wa_lo = sem("s_wa_lo")
        s_wo = sem("s_wo")
        s_wo_n = sem("s_wo_n")
        s_var = sem("s_var")
        s_rstd = sem("s_rstd")
        s_rms = sem("s_rms")
        s_pchain = sem("s_pchain")
        s_xh = sem("s_xh")
        s_ht = sem("s_ht")
        s_chain = sem("s_chain")
        s_nabs = sem("s_nabs")
        s_exp = sem("s_exp")
        s_log = sem("s_log")
        s_ld = sem("s_ld")
        s_nout = sem("s_nout")
        s_htb = [sem(f"s_htb{k}") for k in range(2)]
        s_lg = [sem(f"s_lg{k}") for k in range(2)]
        s_rg = [sem(f"s_rg{k}") for k in range(2)]
        mask_done = sem("mask_done")
        av_done = sem("av_done")
        sq_done = sem("sq_done")
        x_done = sem("x_done")
        s_logits = sem("s_logits")
        s_rexp = sem("s_rexp")
        s_comb = sem("s_comb")
        s_fw = [sem(f"s_fw{k}") for k in range(2)]
        s_fw_hi = sem("s_fw_hi")
        s_fw_lo = sem("s_fw_lo")
        s_wl_raw = sem("s_wl_raw")
        s_wl_hi = sem("s_wl_hi")
        s_wl_lo = sem("s_wl_lo")
        s_ct0 = sem("s_ct0")
        s_qe = sem("s_qe")
        s_qn = sem("s_qn")
        s_kmax = sem("s_kmax")
        s_we = [sem(f"s_we{k}") for k in range(2)]
        s_we_hi = sem("s_we_hi")
        s_we_lo = sem("s_we_lo")
        s_out = sem("s_out")
        link = Chain(s_chain)
        link_pool = Chain(s_pchain)

        U_mod = banks.phase([("modT", 0), ("gates", 1)])

        def boundary_table(routed=True):
            t = []
            for g in range(NG + 1):
                if g < NG:
                    t.append((("tr", g), g % 2))
                if g and routed:
                    t.append((("rt", g - 1), 2 + (g - 1) % 2))
            return t

        U_b = [None] * 4
        U_b[0] = banks.phase(boundary_table())
        U_n = banks.phase([(("n", k), 4 + k) for k in range(4)])

        HALVES = 2 * B
        LOOPED = 12
        PROJ = (("q0", "q1", "g0"), ("g1", "k0", "k1"), ("v0", "v1", "o0", "o1"))
        turn = [0]

        def other(key, name):
            turn[0] += 1
            return ((key, name), 6 + turn[0] % 2)

        def half_table(key, tail, y, proj):
            t = [(key, None)]
            for p in range(3):
                if p == 1 and tail:
                    t += [other(key, "t0"), other(key, "t1")]
                if p == 2 and y:
                    t.append(other(key, "y"))
                if proj:
                    t += [other(key, n) for n in PROJ[p]]
            return t

        base1 = list(banks.base)
        U_p1 = {-1: banks.phase([other(-1, n) for step in PROJ for n in step])}
        U_p1[0] = banks.phase(half_table(0, False, False, True))
        U_p1[1] = banks.phase(half_table(1, True, False, True))
        t = [x for r in range(4) for x in half_table(r, True, r % 2 == 0, True)]
        assert sum(k is not None for _, k in t) % 2 == 0
        U_p1["loop"] = banks.phase(t, LOOPED // 4)
        U_p1[14] = banks.phase(half_table(14, True, True, True))
        U_p1[15] = banks.phase(half_table(15, True, False, False))
        U_p1[16] = banks.phase([other(16, "t0"), other(16, "t1"), other(16, "y")])
        for k in range(4):
            banks.base[k] += 3 * HALVES
        for k in (4, 5):
            banks.base[k] += HALVES
        U_b[1] = banks.phase(boundary_table())

        base2 = list(banks.base)
        if phases >= 2:
            for k in range(6):
                banks.base[k] += (E0 + 1) * NG // 2
        U_b[2] = banks.phase(boundary_table(False))

        def batch_table(key, u, proj):
            here, there = 4 * u, 4 * (1 - u)
            t = [((key, "kT0"), here + 2), ((key, "kT1"), here + 3)]
            t += [((key, "q0"), there), ((key, "q1"), there + 1)] if proj else []
            t += [((key, "qT0"), here), ((key, "qT1"), here + 1)]
            t += [((key, "k0"), there + 2), ((key, "k1"), there + 3)] if proj else []
            t += [((key, "ctx"), here + 2)]
            t += [((key, "v0"), there)] if proj else []
            t += [((key, "m"), here + 3)]
            t += [((key, "v1"), there + 1)] if proj else []
            t += [((key, "y"), here)]
            return t

        U_p3 = {-1: banks.phase([((-1, "q0"), 0), ((-1, "q1"), 1), ((-1, "k0"), 2), ((-1, "k1"), 3),
                                 ((-1, "v0"), 0), ((-1, "v1"), 1)])}
        U_p3["loop"] = banks.phase(batch_table(0, 0, True) + batch_table(1, 1, True), 3)
        U_p3[6] = banks.phase(batch_table(6, 0, True))
        U_p3[7] = banks.phase(batch_table(7, 1, False))
        U_b[3] = banks.phase(boundary_table())
        U_wt = banks.phase([(("wt", g), 4 + g) for g in range(NG)] + [(("b2", g), g) for g in range(NG)])
        base4 = list(banks.base)

        with ExitStack() as stack1:
            def s1(name, shape, dt=F32):
                return sb(name, shape, dt, stack1)

            TRI = s1("TRI", [P, 3 * P])
            WRAW = s1("WRAW", [P, 2, HID0])
            WAH = s1("WAH", [P, 5, HID0], F32R)
            WAL = s1("WAL", [P, 5, HID0], F32R)
            WOR = s1("WOR", [P, HT0, D])
            Z = s1("Z", [P, NT, H0])
            ZA = s1("ZA", [P, NT, H0])
            GS = s1("GS", [B, 4, D])
            GA = s1("GA", [B, 4, D])
            LG = s1("LG", [96, 2, S], F32R)
            RG = s1("RG", [96, 2, HALF, S], F32R)
            Q = s1("Q", [P, 2, 4, S])
            KG = s1("KG", [P, 2, 4, S])
            TG = s1("TG", [P, 2, 2 * S])
            V = s1("V", [P, 2, TT, HALF * DH])
            TO = s1("TO", [P, 2, TT, HALF * DH])
            DB = s1("DB", [P, 2, 2, 512])
            PB = s1("PB", [P, 2, 2, 512])
            SQ = s1("SQ", [P, TT, 512])
            SS = s1("SS", [P, 2, 2, TT])
            SR = s1("SR", [P, 2, TT])
            RMS_C = s1("RMS_C", [P, 2, TT])
            OG = s1("OG", [P, 2, TT, HALF * DH])
            OT = s1("OT", [P, 2, TT, 4, P])
            TMP = s1("TMP", [P, TT, D])

        def s2(name, shape, dt=F32):
            return sb(name, shape, dt)

        ACC = s2("ACC", [P, NT, D])
        SEL = s2("SEL", [P, NT, E0])
        M8 = s2("M8", [P, NT, 8])
        REP = s2("REP", [P, NT, E0])
        SCO = s2("SCO", [P, NT, E0])
        SUM = s2("SUM", [P, NT])
        VAL = s2("VAL", [P, NT, E1 + 6])
        SIL = s2("SIL", [P, 2, GW])
        HB = s2("HB", [P, 2, GW])
        WT = s2("WT", [E1, NT * P])
        WE = s2("WE", [P, 2, 2 * FT * P + FT])
        WEH = s2("WEH", [P, 2, FT * P], F32R)
        WEL = s2("WEL", [P, 2, FT * P], F32R)
        WLR = s2("WLR", [P, 3, HID1])
        WLH = s2("WLH", [P, 3, HID1], F32R)
        WLL = s2("WLL", [P, 3, HID1], F32R)
        WO1 = s2("WO1", [P, HT1, D])
        QM = s2("QM", [P, 2, TT, H1])
        QS = s2("QS", [P, 2, TT, H1])
        QE = s2("QE", [P, 2, TT, HID1])
        QN = s2("QN", [P, 2, TT, HID1])
        KM = s2("KM", [P, 2, HT1])
        KS = s2("KS", [P, 2, HT1])
        RK = s2("RK", [P, 2, HT1])
        KE = s2("KE", [P, 2, HT1, S])
        KT = s2("KT", [P, 2, TT, HID1])
        VV = s2("VV", [P, 2, TT, HID1])
        QT = s2("QT", [P, 2, HT1, S])
        CT = s2("CT", [P, 2, HT1, P])
        MS = s2("MS", [P, 2, HT1, D])
        YT = s2("YT", [P, 2, TT, D])
        HF = s2("HF", [P, 2, FT, GW])

        WM = OG[:, :, :, :].rearrange("p a t n -> p (a t n)")[:, 0:12 * D].rearrange("p (l n) -> p l n", l=2)
        N_HI = TO[0:H0, :, :, :].rearrange("p a t n -> p (a t n)")
        N_LO = V[0:H0, :, :, :].rearrange("p a t n -> p (a t n)")

        def run_halves(eng, half):
            for n in (0, 1):
                half(n, U_p1[n], 0, n, 0, n, 0, n)
            with eng.Fori(0, LOOPED // 4) as i:
                if eng is nc.gpsimd:
                    link_pool.loop(i, 6)
                for r in range(4):
                    half(r, U_p1["loop"], i, 4 * i + (2 + r), 2 * i + (1 + r // 2), r % 2, (1 + r // 2) % 2, 2)
                if eng is nc.gpsimd:
                    link_pool.end(LOOPED // 4)
            for n in (14, 15):
                half(n, U_p1[n], 0, n, 7, n % 2, 1, n)

        def heads_of(kind, par):
            if kind < 2:
                return [(m, 4 * kind + 2 * m + par) for m in range(2)]
            return [(m, 2 * m + par) for m in range(4)]

        block = ctx.enter_context(nc.Block())

        @block.sync
        def _(sp):
            sp.dma_start(M[:, :], misc).then_inc(s_misc, 16)
            sp.dma_start(X[:, 0:GT, :], x_tiles[:, 0:GT, :]).then_inc(s_x[0], 16)
            sp.dma_start(WM, wmod).then_inc(s_mod, 16)
            for g in range(1, NG):
                sp.dma_start(X[:, GT * g:GT * g + GT, :], x_tiles[:, GT * g:GT * g + GT, :]).then_inc(s_x[g], 16)
            for c in range(5):
                if c >= 2:
                    sp.wait_ge(s_wa_lo, c - 1)
                sp.dma_start(WRAW[:, c % 2, :], wa[:, c, :]).then_inc(s_wa_raw[c % 2], 16)
            sp.dma_start(WOR[:, :, :], woT).then_inc(s_wo, 16)
            sp.dma_start(B2[:, :], b2).then_inc(s_wo, 16)
            for k in range(2):
                sp.dma_start(FW[:, k, :, :], w_ffn0[k]).then_inc(s_fw[k], 16)
            sp.wait_ge(s_gates, 1)
            sp.dma_start(gate_scratch.rearrange("l a b d -> b (l a) d"), GS[:, :, :]).then_inc(s_gates_out, 16)
            sp.wait_ge(s_gates_out, 16)
            flat_gb = GB[:, :, :, :].rearrange("p a b d -> p (a b d)")
            sp.dma_start(flat_gb, gate_scratch[0].rearrange("a b d -> (a b d)").partition_broadcast(P)).then_inc(s_gb, 16)

            def load_htb(b, u):
                sp.dma_start(HTB[:, u, :, :].bitcast(F32), HT[:, :, bass.ds(b * S, S)].bitcast(F32)).then_inc(s_htb[u], 16)

            def load_lg(b, u):
                for part in range(2):
                    sp.dma_start(LG[32 + 32 * part:32 + 32 * part + H0, u, :].bitcast(F32),
                                 decay_scratch[part, :, bass.ds(b * S, S)]).then_inc(s_lg[u], 16)

            def load_rg(b, hh):
                sp.dma_start(RG[0:2, hh, :, :].bitcast(F32),
                             decay_scratch[:, hh * HALF:(hh + 1) * HALF, bass.ds(b * S, S)]).then_inc(s_rg[hh], 16)

            if phases >= 1:
                sp.wait_ge(s_ht, 1)
                load_htb(0, 0)
                load_htb(1, 1)
                for k in range(4):
                    sp.wait_ge(emptied[4 + k], U_n.done(("n", k)))
                for part, src in enumerate((N_HI, N_LO)):
                    sp.dma_start(decay_scratch[part], src).then_inc(s_nout, 16)
                sp.wait_ge(s_nout, 32)
                sp.wait_ge(s_rows, 1)
                load_lg(0, 0)
                load_rg(0, 0)
                load_rg(0, 1)
                load_lg(1, 1)

                def half(key, U, i, n, b, hh, u, at_least):
                    if hh == 0 and 1 <= at_least < 14:
                        sp.wait_ge(filled[3], 3 * n + (base1[3] + 1))
                        load_htb(b + 1, 1 - u)
                        load_lg(b + 1, 1 - u)
                    if at_least < 14:
                        sp.wait_ge(filled[1], 3 * n + (base1[1] + 3))
                        load_rg(b + 1, hh)
                run_halves(sp, half)
            if phases >= 2:
                def reload(x, u):
                    sp.wait_ge(s_fw_lo, x + 1)
                    sp.wait_ge(filled[5], 2 * x + (base2[5] + 2))
                    sp.dma_start(FW[:, u, :, :], w_ffn0[bass.ds(x + 2, 1)].rearrange("o p k n -> p (o k) n")).then_inc(s_fw[u], 16)
                reload(0, 0)
                with sp.Fori(0, E0 // 2 - 1) as i:
                    reload(2 * i + 1, 1)
                    reload(2 * i + 2, 0)
            if phases >= 3:
                sp.wait_ge(x_done, B)
                sp.dma_start(WLR[:, :, :], w_l1).then_inc(s_wl_raw, 16)
                sp.dma_start(WO1[:, :, :], wo1).then_inc(s_wl_raw, 16)
                sp.wait_ge(x_done, B + NG)
                sp.dma_start(flat_gb, gate_scratch[1].rearrange("a b d -> (a b d)").partition_broadcast(P)).then_inc(s_gb, 16)
                sp.wait_ge(s_ht, 2 * NG + 1)
                load_htb(0, 0)
                load_htb(1, 1)
                for k in range(2):
                    sp.dma_start(WE[:, k, :], w_ffn1[k]).then_inc(s_we[k], 16)
                if phases == 3:
                    pass

                def batch(key, U, i, b, u):
                    sp.wait_ge(filled[U.bank((key, "y"))], U.done((key, "y"), i))
                    load_htb(b + 2, u)
                with sp.Fori(0, 3) as i:
                    batch(0, U_p3["loop"], i, 2 * i, 0)
                    batch(1, U_p3["loop"], i, 2 * i + 1, 1)
            if phases >= 4:
                def reload4(e, u):
                    sp.wait_ge(s_we_lo, e + 1)
                    sp.wait_ge(filled[5], 2 * e + (base4[5] + 2))
                    sp.dma_start(WE[:, u, :], w_ffn1[bass.ds(e + 2, 1)].rearrange("o p n -> p (o n)")).then_inc(s_we[u], 16)
                with sp.Fori(0, E1 // 2 - 1) as i:
                    reload4(2 * i, 0)
                    reload4(2 * i + 1, 1)
            before = {0: 0, 1: 0, 2: B, 3: B + NG, 4: 2 * B + NG}[phases]
            for g in range(NG):
                if phases in (2, 4):
                    sp.wait_ge(x_done, before + g + 1)
                elif phases:
                    sp.wait_ge(x_done, before + 2 * (g + 1))
                sp.dma_start(out_tiles[:, GT * g:GT * g + GT, :], X[:, GT * g:GT * g + GT, :]).then_inc(s_out, 16)
            sp.wait_ge(s_out, 16 * NG)

        @block.gpsimd
        def _(pool):
            nc.gpsimd.memset(MHALF[:, :], -0.5)
            nc.gpsimd.memset(IDN[:, :], 0.0).then_inc(s_idn, 1)
            pool.wait_ge(s_idn, 1)
            nc.gpsimd.affine_select(out=IDN[:, :], in_=IDN[:, :], compare_op=ALU.not_equal, fill=1.0, base=0,
                                    pattern=[[-1, P]], channel_multiplier=1).then_inc(s_idn, 1)
            nc.gpsimd.memset(TRI[:, 0:P], 0.0)
            nc.gpsimd.memset(TRI[:, P:3 * P], 1.0).then_inc(s_tri, 1)
            pool.wait_ge(s_tri, 1)
            nc.gpsimd.affine_select(out=TRI[:, P:2 * P], in_=TRI[:, P:2 * P], compare_op=ALU.is_ge, fill=0.0, base=0,
                                    pattern=[[1, P]], channel_multiplier=-1).then_inc(s_tri, 1)
            nc.gpsimd.memset(RMS_C[:, 0, :], 4.0 / HID0)
            nc.gpsimd.memset(RMS_C[:, 1, :], 4.0 * RMS_EPS)
            nc.gpsimd.memset(LG[:, :, :].bitcast(F32), 0.0)
            nc.gpsimd.memset(RG[:, :, :, :].bitcast(F32), 0.0).then_inc(s_rows_in, 1)
            pool.wait_ge(s_rows_in, 1)
            for k in range(2):
                for hh in range(2):
                    v = RG[32 + 32 * k:32 + 32 * k + H0, hh, :, :]
                    link_pool(pool, nc.gpsimd.affine_select(
                        out=v, in_=v.bitcast(F32), compare_op=ALU.not_equal, fill=1.0, base=-hh * HALF,
                        pattern=[[-1, HALF], [0, S]], channel_multiplier=1))
            nc.gpsimd.memset(LG[0:2, :, :].bitcast(F32), -1.0).then_inc(s_rows, 1)
            def deviations(k):
                for g in range(NG):
                    pool.wait_ge(s_var, NG * k + g + 1)
                    r = RS[:, GT * g:GT * g + GT]
                    link_pool(pool, nc.gpsimd.tensor_scalar(r, MV[:, GT * g:GT * g + GT, 1], LN_EPS, None, ALU.add))
                    nc.gpsimd.tensor_tensor(r, r, MHALF[:, 0:GT], ALU.pow).then_inc(s_rstd, 1)
            deviations(0)
            for c in range(5):
                pool.wait_ge(s_wa_hi, c + 1)
                nc.gpsimd.tensor_tensor(WAL[:, c, :], WRAW[:, c % 2, :], WAH[:, c, :].bitcast(F32),
                                        ALU.subtract).then_inc(s_wa_lo, 1)
            if phases >= 1:
                def mask(m, par, kind):
                    for e in range(2):
                        pool.wait_ge(emptied[e], m + (base1[e] + 1))
                    if kind < 2:
                        v = DB[:, par, :, :].rearrange("p e (m t) -> p e m t", t=S)[:, :, :, 0:P]
                        pattern = [[0, 2], [0, 2], [1, P - 1]]
                    else:
                        v = DB[:, par, :, :].rearrange("p e (m t) -> p e m t", t=P)
                        pattern = [[0, 2], [0, 4], [1, P - 1]]
                    first, rest = v[:, :, :, 0], v[:, :, :, 1:P]
                    unit = IDN[:, 0:1].unsqueeze(2).to_broadcast(list(first.shape))
                    nc.gpsimd.tensor_tensor(first, unit, unit, ALU.mult).then_inc(mask_done, 1)
                    nc.gpsimd.affine_select(out=rest, in_=rest, compare_op=ALU.is_ge, fill=0.0, base=1, pattern=pattern,
                                            channel_multiplier=-1).then_inc(mask_done, 1)

                def root_mean_squares(n, b, u):
                    pool.wait_ge(sq_done, 2 * n)
                    r = SR[:, u, :]
                    link_pool(pool, nc.gpsimd.tensor_tensor(r, SS[:, u, 0, :], SS[:, u, 1, :], ALU.add))
                    link_pool(pool, nc.gpsimd.tensor_tensor(r, r, RMS_C[:, 0, :], ALU.mult))
                    link_pool(pool, nc.gpsimd.tensor_tensor(r, r, RMS_C[:, 1, :], ALU.add))
                    nc.gpsimd.tensor_tensor(r, r, MHALF[:, 0:TT], ALU.pow).then_inc(s_rms, 1)

                def half(key, U, i, n, b, hh, u, at_least):
                    for p in range(3):
                        mask(3 * n + p, (hh + p) % 2, p)
                        if p == 0 and hh == 0 and at_least >= 2:
                            root_mean_squares(n, b - 1, 1 - u)
                run_halves(pool, half)
                root_mean_squares(16, 7, 1)
                deviations(1)
            if phases >= 2:
                def low(x, u):
                    pool.wait_ge(s_fw_hi, x + 1)
                    nc.gpsimd.tensor_tensor(FWL[:, u, :], FW[:, u, 0:2, :].rearrange("p k n -> p (k n)"),
                                            FWH[:, u, :].bitcast(F32), ALU.subtract).then_inc(s_fw_lo, 1)
                low(0, 0)
                with pool.Fori(0, E0 // 2) as i:
                    low(2 * i + 1, 1)
                    low(2 * i + 2, 0)
                deviations(2)
            if phases >= 3:
                pool.wait_ge(x_done, B)
                nc.gpsimd.memset(CT[:, :, :, :], 0.0).then_inc(s_ct0, 1)
                pool.wait_ge(s_wl_hi, 1)
                nc.gpsimd.tensor_tensor(WLL[:, :, :], WLR[:, :, :], WLH[:, :, :].bitcast(F32), ALU.subtract).then_inc(s_wl_lo, 1)
                deviations(3)
            if phases >= 4:
                def low4(e, u):
                    pool.wait_ge(s_we_hi, e + 1)
                    nc.gpsimd.tensor_tensor(WEL[:, u, :], WE[:, u, 0:FT * P], WEH[:, u, :].bitcast(F32),
                                            ALU.subtract).then_inc(s_we_lo, 1)
                with pool.Fori(0, E1 // 2) as i:
                    low4(2 * i, 0)
                    low4(2 * i + 1, 1)

        @block.scalar
        def _(act):
            def act_boundary(k):
                l, ab = k // 2, k % 2
                U = U_b[k]
                for g in range(NG):
                    act.wait_ge(filled[U.bank(("tr", g))], U.done(("tr", g)))
                    for h in range(2):
                        b = 2 * g + h
                        a = nc.scalar.activation(H32[:, g % 2, S * h:S * h + S],
                                                 bank[U.bank(("tr", g))][:, S * h:S * h + S], ACT.Identity,
                                                 scale=MODT[:, l, 2 * ab + 1, b:b + 1], bias=MODT[:, l, 2 * ab, b:b + 1])
                    a.then_inc(emptied[U.bank(("tr", g))], 1)

            act.wait_ge(s_misc, 16)
            nc.scalar.activation(SC[:, :, :].rearrange("p l b -> p (l b)"), misc_of("c"), ACT.Silu).then_inc(s_silu, 1)
            act.wait_ge(emptied[0], U_mod.done("modT"))
            act_boundary(0)
            for c in range(5):
                act.wait_ge(s_wa_raw[c % 2], 16 * (c // 2 + 1))
                nc.scalar.activation(WAH[:, c, :], WRAW[:, c % 2, :], ACT.Copy).then_inc(s_wa_hi, 1)
            act.wait_ge(s_nabs, 1)
            za = ZA[:, :, :].rearrange("p t h -> p (t h)")
            nc.scalar.activation(za, za, ACT.Exp).then_inc(s_exp, 1)
            act.wait_ge(s_exp, 1)
            nc.scalar.activation(za, za, ACT.Ln, bias=1.0).then_inc(s_log, 1)

            if phases >= 1:
                def project(key, U, i, hh, name, out_, func, scale):
                    k = U.bank((key, name))
                    act.wait_ge(filled[k], U.done((key, name), i))
                    nc.scalar.activation(out_, bank[k][:, :], func, scale=scale).then_inc(emptied[k], 1)

                def projections(key, U, i, hh, names):
                    for name in names:
                        j = int(name[1])
                        if name[0] == "q":
                            project(key, U, i, hh, name, Q[:, hh, 2 * j:2 * j + 2, :].rearrange("p m t -> p (m t)"),
                                    ACT.Copy, 0.5)
                        elif name[0] == "g":
                            project(key, U, i, hh, name, TG[:, j, :], ACT.Tanh, 0.5)
                        elif name[0] == "o":
                            project(key, U, i, hh, name, TO[:, hh, j, :], ACT.Tanh, 0.5)

                def decays(m, par, at_least):
                    if at_least >= 2:
                        for e in range(2):
                            act.wait_ge(emptied[2 + e], m + (base1[2 + e] - 1))
                    for e in range(2):
                        act.wait_ge(filled[e], m + (base1[e] + 1))
                        nc.scalar.activation(DB[:, par, e, :], bank[e][:, :], ACT.Exp).then_inc(emptied[e], 1)

                def squares(n, hh, u, at_least):
                    for t in range(TT):
                        if at_least >= 1:
                            act.wait_ge(sq_done, 2 * n + (t - 1))
                        act.wait_ge(filled[4 + t], n + (base1[4 + t] + 1))
                        nc.scalar.activation(SQ[:, t, :], bank[4 + t][:, :], ACT.Square,
                                             accum_out=SS[:, u, hh, t:t + 1]).then_inc(sq_done, 1)

                def outputs_turned(key, U, i, hh):
                    for t in range(TT):
                        k = U.bank((key, f"t{t}"))
                        act.wait_ge(filled[k], U.done((key, f"t{t}"), i))
                        nc.scalar.activation(OT[:, hh, t, :, :].rearrange("p j n -> p (j n)"), bank[k][:, :],
                                             ACT.Copy).then_inc(emptied[k], 1)

                def half(key, U, i, n, b, hh, u, at_least):
                    for p in range(3):
                        if p == 1 and at_least >= 1:
                            outputs_turned(key, U, i, 1 - hh)
                        if at_least < 15:
                            projections(key, U, i, 1 - hh, PROJ[p])
                        if at_least < 15 or p < 2:
                            decays(3 * n + (p + 1), (hh + p + 1) % 2, 3 * at_least + p + 1)
                    squares(n, hh, u, at_least)
                act.wait_ge(s_nout, 32)
                for names in PROJ:
                    projections(-1, U_p1[-1], 0, 0, names)
                decays(0, 0, 0)
                run_halves(act, half)
                outputs_turned(16, U_p1[16], 0, 1)
                act_boundary(1)
                for g in (NG - 2, NG - 1):
                    act.wait_ge(emptied[U_b[1].bank(("rt", g))], U_b[1].done(("rt", g)))
                nc.scalar.activation(REP[:, :, :], SCO[:, :, :], ACT.Exp, scale=-1.0).then_inc(s_rexp, 1)
            if phases >= 2:
                def high(x, u, loads):
                    act.wait_ge(s_fw[u], loads)
                    nc.scalar.activation(FWH[:, u, :], FW[:, u, 0:2, :].rearrange("p k n -> p (k n)"),
                                         ACT.Copy).then_inc(s_fw_hi, 1)

                def gate_step(x, g, first=False):
                    k = g % 2
                    act.wait_ge(filled[k], 2 * x + (base2[k] + g // 2 + 1))
                    if not (first and g < 2):
                        act.wait_ge(emptied[2 + k], 2 * x + (base2[2 + k] + g // 2))
                    nc.scalar.activation(SIL[:, k, :], bank[k][:, :], ACT.Silu).then_inc(emptied[k], 1)

                def expert(x, u, loads, at_least):
                    for g in range(NG):
                        gate_step(x, g, at_least == 0)
                        if g == 0 and at_least < E0:
                            high(x + 1, 1 - u, loads)

                high(0, 0, 16)
                expert(0, 0, 16, 0)
                with act.Fori(0, E0 // 2 - 1) as i:
                    expert(2 * i + 1, 1, 16 * i + 32, 1)
                    expert(2 * i + 2, 0, 16 * i + 32, 1)
                expert(E0 - 1, 1, 16 * (E0 // 2 + 1), E0 - 1)
                expert(E0, 0, 0, E0)
                act_boundary(2)
            if phases >= 3:
                act.wait_ge(s_wl_raw, 32)
                nc.scalar.activation(WLH[:, :, :], WLR[:, :, :], ACT.Copy).then_inc(s_wl_hi, 1)

                def q_exp(b, u, t):
                    k = 4 * u + t
                    nc.scalar.activation(QE[:, u, t, :], QE[:, u, t, :], ACT.Exp).then_inc(s_qe, 1)

                def batch(key, U, i, b, u, tail, proj):
                    def copy_out(name, out_):
                        k = U.bank((key, name))
                        act.wait_ge(filled[k], U.done((key, name), i))
                        nc.scalar.activation(out_, bank[k][:, :], ACT.Copy).then_inc(emptied[k], 1)

                    v = 1 - u
                    if tail:
                        for t in range(TT):
                            copy_out(f"kT{t}", KT[:, u, t, :])
                    if proj:
                        for t in range(TT):
                            k = U.bank((key, f"q{t}"))
                            act.wait_ge(emptied[k], U.done((key, f"q{t}"), i))
                            nc.scalar.activation(QE[:, v, t, :], QE[:, v, t, :], ACT.Exp).then_inc(s_qe, 1)
                    if tail:
                        for t in range(2):
                            copy_out(f"qT{t}", QT[:, u, 2 * t:2 * t + 2, :].rearrange("p j t -> p (j t)"))
                    if proj:
                        for j in range(2):
                            k = U.bank((key, f"k{j}"))
                            act.wait_ge(s_kmax, 2 * b + (3 + j))
                            for h in range(2):
                                a = nc.scalar.activation(KE[:, v, 2 * j + h, :], bank[k][:, S * h:S * h + S], ACT.Exp,
                                                         bias=KM[:, v, 2 * j + h:2 * j + h + 1],
                                                         accum_out=KS[:, v, 2 * j + h:2 * j + h + 1])
                            a.then_inc(emptied[k], 1)
                        for t in range(TT):
                            copy_out(f"v{t}", VV[:, v, t, :])

                batch(-1, U_p3[-1], 0, -1, 1, False, True)
                with act.Fori(0, 3) as i:
                    batch(0, U_p3["loop"], i, 2 * i, 0, True, True)
                    batch(1, U_p3["loop"], i, 2 * i + 1, 1, True, True)
                batch(6, U_p3[6], 0, 6, 0, True, True)
                batch(7, U_p3[7], 0, 7, 1, True, False)
                act_boundary(3)
                act.wait_ge(s_logits, 1)
                nc.scalar.activation(SCO[:, :, 0:E1], SCO[:, :, 0:E1], ACT.Exp).then_inc(s_rexp, 1)
            if phases >= 4:
                def high4(e, u, loads):
                    act.wait_ge(s_we[u], loads)
                    nc.scalar.activation(WEH[:, u, :], WE[:, u, 0:FT * P], ACT.Copy).then_inc(s_we_hi, 1)

                def expert4(e, u, loads, at_least):
                    for g in range(NG):
                        k = g % 2
                        for f in range(FT):
                            act.wait_ge(filled[f], 4 * e + (base4[f] + g + 1))
                            if f == 0 and not (at_least == 0 and g < 2):
                                act.wait_ge(filled[4 + k], 2 * e + (base4[4 + k] + g // 2))
                            nc.scalar.activation(HF[:, k, f, :], bank[f][:, :], ACT.Relu,
                                                 bias=WE[:, u, 2 * FT * P + f:2 * FT * P + f + 1]).then_inc(emptied[f], 1)
                        if g == 0 and at_least < E1 - 1:
                            high4(e + 1, 1 - u, loads)

                high4(0, 0, 16)
                expert4(0, 0, 16, 0)
                with act.Fori(0, E1 // 2 - 1) as i:
                    expert4(2 * i + 1, 1, 16 * i + 32, 1)
                    expert4(2 * i + 2, 0, 16 * i + 32, 1)
                expert4(E1 - 1, 1, 0, E1 - 1)

        @block.vector
        def _(dve):
            def layer_norm(k, g):
                for t in range(GT * g, GT * g + GT):
                    a = nc.vector.bn_stats(out=ST[:, t, :], in_=X[:, t, :])
                link(dve, a)
                for t in range(GT * g, GT * g + GT):
                    a = nc.vector.bn_aggr(out=MV[:, t, :], in_=ST[:, t, :])
                a.then_inc(s_var, 1)
                dve.wait_ge(s_rstd, NG * k + g + 1)
                for t in range(GT * g, GT * g + GT):
                    a = nc.vector.tensor_scalar(XH[:, g % 2, t - GT * g, :], X[:, t, :], MV[:, t, 0:1], RS[:, t:t + 1],
                                                ALU.subtract, ALU.mult)
                a.then_inc(s_xh, 1)

            def combine(ab, g, ready, value, count):
                dve.wait_ge(ready, value)
                for h in range(2):
                    v = ACC[:, GT * g + TT * h:GT * g + TT * h + TT, :]
                    gb = GB[:, ab, 2 * g + h, :].unsqueeze(1).to_broadcast([P, TT, D])
                    a = nc.vector.tensor_tensor(v, v, gb, ALU.mult)
                link(dve, a)
                v = X[:, GT * g:GT * g + GT, :]
                nc.vector.tensor_tensor(v, v, ACC[:, GT * g:GT * g + GT, :], ALU.add).then_inc(x_done, 1)
                dve.wait_ge(x_done, count)

            def boundary(k, before, take):
                U = U_b[k]
                for g in range(NG + 1):
                    if g < NG:
                        before(g)
                        layer_norm(k, g)
                    if g:
                        q = g - 1
                        tr = U.bank(("tr", q))
                        dve.wait_ge(emptied[tr], U.done(("tr", q)))
                        hi = HT[:, 0, GW * q:GW * q + GW]
                        link(dve, nc.vector.tensor_copy(hi, H32[:, q % 2, :]))
                        nc.vector.tensor_tensor(HT[:, 1, GW * q:GW * q + GW], H32[:, q % 2, :], hi.bitcast(F32),
                                                ALU.subtract).then_inc(s_ht, 1)
                        if take is not None:
                            rt = U.bank(("rt", q))
                            dve.wait_ge(filled[rt], U.done(("rt", q)))
                            take(slice(GT * q, GT * q + GT), bank[rt]).then_inc(emptied[rt], 1)
                            dve.wait_ge(emptied[rt], U.done(("rt", q)))

            dve.wait_ge(filled[0], U_mod.done("modT"))
            link(dve, nc.vector.tensor_copy(MODT[:, :, :, :].rearrange("p l q b -> p (l q b)"), bank[0][:, 0:8 * B]))
            v = MODT[:, :, :, :].rearrange("p l (a q) b -> p (l a) q b", q=2)[:, :, 1, :]
            nc.vector.tensor_scalar_add(v, v, 1.0).then_inc(emptied[0], 1)
            dve.wait_ge(filled[1], U_mod.done("gates"))
            gates = bank[1][0:B, :]
            ga = GA[:, :, :].rearrange("b k d -> b (k d)")
            gs = GS[:, :, :].rearrange("b k d -> b (k d)")
            nc.vector.tensor_scalar(gs, gates, 0.0, 2.0, ALU.is_ge, ALU.mult)
            link(dve, nc.vector.tensor_scalar(ga, gates, 0.25, None, ALU.max))
            nc.vector.scalar_tensor_tensor(ga, gates, -1.0, ga, ALU.mult, ALU.max).then_inc(emptied[1], 1)
            dve.wait_ge(emptied[1], U_mod.done("gates"))
            nc.vector.scalar_tensor_tensor(gs, gs, 1.0, ga, ALU.subtract, ALU.mult).then_inc(s_gates, 1)

            def take_decay(tiles, b_):
                return nc.vector.tensor_tensor(Z[:, tiles, :], b_[:, 0:GT * H0].rearrange("p (t h) -> p t h", h=H0),
                                               misc_of("bd").unsqueeze(1).to_broadcast([P, GT, H0]), ALU.add)
            boundary(0, lambda g: dve.wait_ge(s_x[g], 16), take_decay)
            z = Z[:, :, :].rearrange("p t h -> p (t h)")
            za = ZA[:, :, :].rearrange("p t h -> p (t h)")
            nc.vector.scalar_tensor_tensor(za, z, -1.0, z, ALU.mult, ALU.min).then_inc(s_nabs, 1)
            dve.wait_ge(s_wo, 32)
            nc.vector.tensor_tensor(WOR[:, :, :], WOR[:, :, :], misc_of("norm_w").unsqueeze(2).to_broadcast([P, HT0, D]),
                                    ALU.mult).then_inc(s_wo_n, 1)
            dve.wait_ge(s_log, 1)
            nc.vector.scalar_tensor_tensor(z, z, 0.0, za, ALU.max, ALU.add).then_inc(s_ld, 1)
            for k in range(4):
                dve.wait_ge(filled[4 + k], U_n.done(("n", k)))
                hi = N_HI[:, 512 * k:512 * k + 512]
                link(dve, nc.vector.tensor_copy(hi.bitcast(F32R), bank[4 + k][0:H0, :]))
                nc.vector.tensor_tensor(N_LO[:, 512 * k:512 * k + 512].bitcast(F32R), bank[4 + k][0:H0, :], hi,
                                        ALU.subtract).then_inc(emptied[4 + k], 1)

            if phases >= 1:
                dve.wait_ge(s_gb, 16)

                def projections(key, U, i, hh, names):
                    for name in names:
                        j, k = int(name[1]), U.bank((key, name)) if name[0] in "kv" else None
                        if name[0] == "k":
                            g = U.bank((key, f"g{j}"))
                            dve.wait_ge(emptied[g], U.done((key, f"g{j}"), i))
                            dve.wait_ge(filled[k], U.done((key, name), i))
                            nc.vector.scalar_tensor_tensor(
                                KG[:, hh, 2 * j:2 * j + 2, :].rearrange("p m t -> p (m t)"), TG[:, j, :], 1.0,
                                bank[k][:, :], ALU.add, ALU.mult).then_inc(emptied[k], 1)
                        elif name[0] == "v":
                            dve.wait_ge(filled[k], U.done((key, name), i))
                            nc.vector.tensor_copy(V[:, hh, j, :], bank[k][:, :]).then_inc(emptied[k], 1)

                def weigh(n, hh, p):
                    m, par = 3 * n + p, (hh + p) % 2
                    dve.wait_ge(mask_done, 2 * m + 2)
                    if p == 0:
                        dve.wait_ge(av_done, 2 * n)
                    elif p == 1:
                        dve.wait_ge(filled[5], n + base1[5])
                    else:
                        dve.wait_ge(av_done, 2 * n + 1)
                    for e in range(2):
                        dve.wait_ge(filled[2 + e], m + (base1[2 + e] + 1))
                        nc.vector.tensor_tensor(PB[:, par, e, :], bank[2 + e][:, :], DB[:, par, e, :],
                                                ALU.mult).then_inc(emptied[2 + e], 1)

                def gate_outputs(n, hh):
                    dve.wait_ge(sq_done, 2 * n + 2)
                    for t in range(TT):
                        nc.vector.scalar_tensor_tensor(OG[:, hh, t, :], TO[:, hh, t, :], 1.0, bank[4 + t][:, :],
                                                       ALU.add, ALU.mult).then_inc(emptied[4 + t], 1)

                def add_attention(key, U, i, b, u):
                    dve.wait_ge(s_rms, b + 1)
                    k = U.bank((key, "y"))
                    dve.wait_ge(filled[k], U.done((key, "y"), i))
                    for t in range(TT):
                        a = nc.vector.scalar_tensor_tensor(TMP[:, t:t + 1, :], bank[k][:, D * t:D * t + D].unsqueeze(1),
                                                           SR[:, u, t:t + 1], GB[:, 0, bass.ds(b, 1), :],
                                                           ALU.mult, ALU.mult)
                    a.then_inc(emptied[k], 1)
                    dve.wait_ge(emptied[k], U.done((key, "y"), i))
                    v = X[:, bass.ds(TT * b, TT), :]
                    nc.vector.tensor_tensor(v, v, TMP[:, :, :], ALU.add).then_inc(x_done, 1)

                def half(key, U, i, n, b, hh, u, at_least):
                    for p in range(3):
                        weigh(n, hh, p)
                        if p == 0 and at_least >= 1:
                            gate_outputs(n - 1, 1 - hh)
                        if p == 2 and hh == 0 and at_least >= 2:
                            add_attention(key, U, i, b - 1, 1 - u)
                        if at_least < 15:
                            projections(key, U, i, 1 - hh, PROJ[p])

                dve.wait_ge(s_nout, 32)
                for names in PROJ:
                    projections(-1, U_p1[-1], 0, 0, names)
                run_halves(dve, half)
                gate_outputs(15, 1)
                add_attention(16, U_p1[16], 0, 7, 1)

                def take_logits(tiles, b_):
                    return nc.vector.tensor_copy(SCO[:, tiles, :], b_[:, 0:GT * E0].rearrange("p (t e) -> p t e", e=E0))
                nc.vector.memset(COMB[:, :, 0:1], 1.0)
                boundary(1, lambda g: dve.wait_ge(x_done, 2 * g + 2), take_logits)
                dve.wait_ge(s_rexp, 1)
                bc = [P, NT, E0]
                link(dve, nc.vector.tensor_scalar_add(REP[:, :, :], REP[:, :, :], 1.0))
                link(dve, nc.vector.reciprocal(SCO[:, :, :], REP[:, :, :]))
                link(dve, nc.vector.tensor_tensor(SEL[:, :, :], SCO[:, :, :], misc_of("ebias").unsqueeze(1).to_broadcast(bc),
                                                  ALU.add))
                for t in range(NT):
                    a = nc.vector.max(out=M8[:, t, :], in_=SEL[:, t, :])
                link(dve, a)
                for t in range(NT):
                    a = nc.vector.match_replace(out=REP[:, t, :], in_to_replace=M8[:, t, :], in_values=SEL[:, t, :],
                                                imm_value=-BIG)
                link(dve, a)
                link(dve, nc.vector.tensor_tensor(REP[:, :, :], REP[:, :, :], SEL[:, :, :], ALU.not_equal))
                link(dve, nc.vector.tensor_tensor(REP[:, :, :], REP[:, :, :], SCO[:, :, :], ALU.mult))
                link(dve, nc.vector.tensor_reduce(out=SUM[:, :], in_=REP[:, :, :], axis=AX_X, op=ALU.add))
                link(dve, nc.vector.reciprocal(SUM[:, :], SUM[:, :]))
                link(dve, nc.vector.tensor_scalar(SUM[:, :], SUM[:, :], ROUTE_SCALE, None, ALU.mult))
                link(dve, nc.vector.tensor_tensor(COMB[:, :, 1:E0 + 1], REP[:, :, :],
                                                  SUM[:, :].unsqueeze(2).to_broadcast(bc), ALU.mult))
            if phases >= 2:
                link(dve, nc.vector.memset(ACC[:, :, :], 0.0))

                def add_expert(x, g, y, y_base, per, at_least):
                    k = y + g % 2
                    dve.wait_ge(filled[k], 2 * x + (y_base[k] + g // 2 + 1))
                    if at_least:
                        dve.wait_ge(emptied[k], 2 * x + (y_base[k] + g // 2 - 1))
                    for t in range(GT):
                        v = ACC[:, GT * g + t, :]
                        a = nc.vector.scalar_tensor_tensor(v, bank[k][:, D * t:D * t + D],
                                                           COMB[:, GT * g + t, bass.ds(x, 1)], v, ALU.mult, ALU.add)
                    a.then_inc(emptied[k], 1)

                def hidden(x, g, at_least):
                    k = g % 2
                    dve.wait_ge(emptied[k], 2 * x + (base2[k] + g // 2 + 1))
                    dve.wait_ge(filled[2 + k], 2 * x + (base2[2 + k] + g // 2 + 1))
                    if at_least or g >= 2:
                        dve.wait_ge(filled[4 + k], 2 * x + (base2[4 + k] + g // 2))
                    nc.vector.tensor_tensor(HB[:, k, :], SIL[:, k, :], bank[2 + k][:, :], ALU.mult).then_inc(emptied[2 + k], 1)

                def expert(x, at_least):
                    for g in range(NG):
                        hidden(x, g, at_least)
                        if g:
                            add_expert(x, g - 1, 4, base2, 0, at_least)
                        elif at_least:
                            add_expert(x - 1, NG - 1, 4, base2, 0, at_least - 1)

                expert(0, 0)
                expert(1, 1)
                with dve.Fori(0, (E0 - 2) // 2) as i:
                    expert(2 * i + 2, 2)
                    expert(2 * i + 3, 2)
                expert(E0, 2)
                add_expert(E0, NG - 1, 4, base2, 0, 1)
                boundary(2, lambda g: combine(1, g, emptied[4 + g % 2], base2[4 + g % 2] + 2 * E0 + g // 2 + 1, B + g + 1), None)
            if phases >= 3:
                def q_scores(key, U, i, v, t):
                    k = U.bank((key, f"q{t}"))
                    dve.wait_ge(filled[k], U.done((key, f"q{t}"), i))
                    q = bank[k][:, :].rearrange("p (h d) -> p h d", d=DH)
                    link(dve, nc.vector.tensor_reduce(out=QM[:, v, t, :], in_=q, axis=AX_X, op=ALU.max))
                    nc.vector.tensor_tensor(QE[:, v, t, :].rearrange("p (h d) -> p h d", d=DH), q,
                                            QM[:, v, t, :].unsqueeze(2).to_broadcast([P, H1, DH]),
                                            ALU.subtract).then_inc(emptied[k], 1)

                def q_normed(b, v, t):
                    dve.wait_ge(s_qe, 2 * b + (t + 1))
                    e = QE[:, v, t, :].rearrange("p (h d) -> p h d", d=DH)
                    link(dve, nc.vector.tensor_reduce(out=QS[:, v, t, :], in_=e, axis=AX_X, op=ALU.add))
                    link(dve, nc.vector.reciprocal(QS[:, v, t, :], QS[:, v, t, :]))
                    nc.vector.tensor_tensor(QN[:, v, t, :].rearrange("p (h d) -> p h d", d=DH), e,
                                            QS[:, v, t, :].unsqueeze(2).to_broadcast([P, H1, DH]),
                                            ALU.mult).then_inc(s_qn, 1)

                def batch(key, U, i, b, u, tail, proj):
                    v = 1 - u
                    if proj:
                        for t in range(TT):
                            q_scores(key, U, i, v, t)
                        for j in range(2):
                            k = U.bank((key, f"k{j}"))
                            dve.wait_ge(filled[k], U.done((key, f"k{j}"), i))
                            link(dve, nc.vector.tensor_reduce(out=KM[:, v, 2 * j:2 * j + 2],
                                                              in_=bank[k][:, :].rearrange("p (j t) -> p j t", t=S),
                                                              axis=AX_X, op=ALU.max))
                            nc.vector.tensor_scalar(KM[:, v, 2 * j:2 * j + 2], KM[:, v, 2 * j:2 * j + 2], -1.0, None,
                                                    ALU.mult).then_inc(s_kmax, 1)
                    if tail:
                        k = U.bank((key, "ctx"))
                        dve.wait_ge(filled[k], U.done((key, "ctx"), i))
                        c = bank[k][:, :].rearrange("p (j n) -> p j n", n=P)
                        nc.vector.tensor_copy(CT[0:DH, u, :, 0:DH], c[0:DH, :, 0:DH])
                        nc.vector.tensor_copy(CT[DH:P, u, :, DH:P], c[DH:P, :, DH:P]).then_inc(emptied[k], 1)
                        link(dve, nc.vector.reciprocal(RK[:, u, :], KS[:, u, :]))
                        link(dve, nc.vector.tensor_scalar(RK[:, u, :], RK[:, u, :], DH ** -0.5, None, ALU.mult))
                    if proj:
                        q_normed(b + 1, v, 0)
                    if tail:
                        k = U.bank((key, "m"))
                        dve.wait_ge(filled[k], U.done((key, "m"), i))
                        nc.vector.tensor_tensor(MS[:, u, :, :], bank[k][:, :].rearrange("p (j n) -> p j n", n=D),
                                                RK[:, u, :].unsqueeze(2).to_broadcast([P, HT1, D]),
                                                ALU.mult).then_inc(emptied[k], 1)
                    if proj:
                        q_normed(b + 1, v, 1)
                    if tail:
                        k = U.bank((key, "y"))
                        dve.wait_ge(filled[k], U.done((key, "y"), i))
                        nc.vector.tensor_tensor(YT[:, u, :, :], bank[k][:, 0:TT * D].rearrange("p (t d) -> p t d", d=D),
                                                misc_of("bo").unsqueeze(1).to_broadcast([P, TT, D]),
                                                ALU.add).then_inc(emptied[k], 1)
                        dve.wait_ge(emptied[k], U.done((key, "y"), i))
                        link(dve, nc.vector.tensor_tensor(YT[:, u, :, :], YT[:, u, :, :],
                                                          GB[:, 0, bass.ds(b, 1), :].to_broadcast([P, TT, D]), ALU.mult))
                        x_ = X[:, bass.ds(TT * b, TT), :]
                        nc.vector.tensor_tensor(x_, x_, YT[:, u, :, :], ALU.add).then_inc(x_done, 1)

                dve.wait_ge(s_gb, 32)
                dve.wait_ge(s_ct0, 1)
                batch(-1, U_p3[-1], 0, -1, 1, False, True)
                with dve.Fori(0, 3) as i:
                    link.loop(i, 22)
                    batch(0, U_p3["loop"], i, 2 * i, 0, True, True)
                    batch(1, U_p3["loop"], i, 2 * i + 1, 1, True, True)
                    link.end(3)
                batch(6, U_p3[6], 0, 6, 0, True, True)
                batch(7, U_p3[7], 0, 7, 1, True, False)

                def take_logits1(tiles, b_):
                    return nc.vector.tensor_tensor(VAL[:, tiles, 0:E1], b_[:, 0:GT * E1].rearrange("p (t e) -> p t e", e=E1),
                                                   misc_of("b_router").unsqueeze(1).to_broadcast([P, GT, E1]), ALU.add)
                nc.vector.memset(VAL[:, :, E1:E1 + 6], BIG)
                boundary(3, lambda g: dve.wait_ge(x_done, B + NG + 2 * g + 2), take_logits1)
                for t in range(NT):
                    a = nc.vector.max(out=M8[:, t, :], in_=VAL[:, t, :])
                link(dve, a)
                nc.vector.tensor_tensor(SCO[:, :, 0:E1], VAL[:, :, 0:E1], M8[:, :, 6:7].to_broadcast([P, NT, E1]),
                                        ALU.subtract).then_inc(s_logits, 1)
                for t in range(NT):
                    a = nc.vector.match_replace(out=REP[:, t, 0:E1 + 6], in_to_replace=M8[:, t, :], in_values=VAL[:, t, :],
                                                imm_value=-BIG)
                link(dve, a)
                link(dve, nc.vector.tensor_tensor(SEL[:, :, 0:E1], REP[:, :, 0:E1], VAL[:, :, 0:E1], ALU.not_equal))
                dve.wait_ge(s_rexp, 2)
                link(dve, nc.vector.tensor_tensor(SEL[:, :, 0:E1], SEL[:, :, 0:E1], SCO[:, :, 0:E1], ALU.mult))
                link(dve, nc.vector.tensor_reduce(out=SUM[:, :], in_=SEL[:, :, 0:E1], axis=AX_X, op=ALU.add))
                link(dve, nc.vector.reciprocal(SUM[:, :], SUM[:, :]))
                nc.vector.tensor_tensor(COMB[:, :, 0:E1], SEL[:, :, 0:E1], SUM[:, :].unsqueeze(2).to_broadcast([P, NT, E1]),
                                        ALU.mult).then_inc(s_comb, 1)
            if phases >= 4:
                for g in range(NG):
                    dve.wait_ge(filled[4 + g], U_wt.done(("wt", g)))
                    nc.vector.tensor_copy(WT[:, GW * g:GW * g + GW], bank[4 + g][0:E1, :]).then_inc(emptied[4 + g], 1)
                for g in range(NG):
                    dve.wait_ge(filled[g], U_wt.done(("b2", g)))
                    nc.vector.tensor_copy(ACC[:, GT * g:GT * g + GT, :].rearrange("p t d -> p (t d)"),
                                          bank[g][:, :]).then_inc(emptied[g], 1)
                for g in range(NG):
                    dve.wait_ge(emptied[g], U_wt.done(("b2", g)))

                def expert4(e, at_least):
                    for g in range(NG):
                        if g:
                            add_expert(e, g - 1, 4, base4, 0, at_least)
                        elif at_least:
                            add_expert(e - 1, NG - 1, 4, base4, 0, at_least - 1)
                expert4(0, 0)
                expert4(1, 1)
                with dve.Fori(0, (E1 - 2) // 2) as i:
                    expert4(2 * i + 2, 2)
                    expert4(2 * i + 3, 2)
                add_expert(E1 - 1, NG - 1, 4, base4, 0, 1)
                for g in range(NG):
                    combine(1, g, emptied[4 + g % 2], base4[4 + g % 2] + 2 * (E1 - 1) + g // 2 + 1, 2 * B + NG + g + 1)

        @block.tensor
        def _(pe):
            def mm(out_, lhsT, rhs, start, stop, **kw):
                return nc.tensor.matmul(out_, lhsT, rhs, start=start, stop=stop, **kw)

            def open_bank(U, name, i=0):
                k = U.bank(name)
                pe.wait_ge(emptied[k], U.free(name, i))
                return k

            def split_product(out_, lhsT, rhs):
                for n, (a, b_) in enumerate(((0, 0), (0, 1), (1, 0))):
                    last = mm(out_, lhsT(a), rhs(b_), n == 0, n == 2)
                return last

            pe.wait_ge(s_silu, 1)
            pe.wait_ge(s_mod, 16)
            for l in range(2):
                for q, part in enumerate((0, 1, 3, 4)):
                    a = mm(bank[0][:, (4 * l + q) * B:(4 * l + q + 1) * B], WM[:, l, part * D:part * D + D], SC[:, l, :],
                           True, True)
            a.then_inc(filled[0], 1)
            for l in range(2):
                for q, part in enumerate((2, 5)):
                    a = mm(bank[1][0:B, (2 * l + q) * D:(2 * l + q + 1) * D], SC[:, l, :], WM[:, l, part * D:part * D + D],
                           True, True)
            a.then_inc(filled[1], 1)

            def boundary(k, weights, width):
                U = U_b[k]
                for g in range(NG + 1):
                    if g < NG:
                        pe.wait_ge(s_xh, NG * k + g + 1)
                        b_ = open_bank(U, ("tr", g))
                        for t in range(GT):
                            a = nc.tensor.transpose(bank[b_][:, P * t:P * t + P], XH[:, g % 2, t, :], IDN[:, :])
                        a.then_inc(filled[b_], 1)
                    if g and weights is not None:
                        q = g - 1
                        tr = U.bank(("tr", q))
                        pe.wait_ge(emptied[tr], U.done(("tr", q)))
                        b_ = open_bank(U, ("rt", q))
                        for t in range(GT):
                            a = mm(bank[b_][:, width * t:width * t + width], H32[:, q % 2, P * t:P * t + P], weights,
                                   True, True)
                        a.then_inc(filled[b_], 1)

            pe.wait_ge(s_idn, 2)
            pe.wait_ge(s_misc, 16)
            boundary(0, misc_of("wd"), H0)
            pe.wait_ge(s_ld, 1)
            pe.wait_ge(s_tri, 2)
            for k in range(4):
                b_ = open_bank(U_n, ("n", k))
                for h in range(2):
                    for c in range(TT):
                        a = mm(bank[b_][0:H0, S * h:S * h + S], Z[:, 2 * (2 * k + h) + c, :],
                               TRI[:, P - P * c:P - P * c + S], c == 0, c == 1)
                a.then_inc(filled[b_], 1)

            if phases >= 1:
                def projections(key, U, i, hh, u, names):
                    for name in names:
                        what, j = "qkvgo".index(name[0]), int(name[1])
                        k = open_bank(U, (key, name), i)
                        w = (WAH, WAL)
                        if name[0] in "qkg":
                            for m in range(2):
                                c = (4 * hh + 2 * j + m) * P
                                a = split_product(bank[k][:, S * m:S * m + S], lambda p_: w[p_][:, what, c:c + P],
                                                  lambda p_: HTB[:, u, p_, :])
                        else:
                            c = hh * HALF * DH
                            a = split_product(bank[k][:, :], lambda p_: HTB[:, u, p_, P * j:P * j + P],
                                              lambda p_: w[p_][:, what, c:c + HALF * DH])
                        a.then_inc(filled[k], 1)

                def arguments(m, kind, hh, u, lg_loads, rg_loads):
                    pe.wait_ge(s_lg[u], lg_loads)
                    pe.wait_ge(s_rg[hh], rg_loads)
                    v = RG[:, hh, :, :].rearrange("k (h two) t -> k two h t", two=2)
                    for e in range(2):
                        pe.wait_ge(emptied[e], m + base1[e])
                        if kind < 2:
                            a = mm(bank[e][:, :], LG[:, u, 0:P], v[:, e, 2 * kind:2 * kind + 2, :], True, True)
                        else:
                            a = mm(bank[e][:, :], LG[:, u, P:S], v[:, e, :, P:S], True, True)
                        a.then_inc(filled[e], 1)

                def scores(m, kind, hh):
                    for e in range(2):
                        pe.wait_ge(emptied[2 + e], m + base1[2 + e])
                    steps = 2 if kind < 2 else 4
                    for n in range(steps):
                        for e in range(2):
                            r = slice(DH * e, DH * e + DH)
                            if kind < 2:
                                j = 2 * kind + n
                                a = mm(bank[2 + e][:, S * n:S * n + S], KG[r, hh, j, 0:P], Q[r, hh, j, :], True, True)
                            else:
                                a = mm(bank[2 + e][:, P * n:P * n + P], KG[r, hh, n, P:S], Q[r, hh, n, P:S], True, True)
                            if n == steps - 1:
                                a.then_inc(filled[2 + e], 1)

                def outputs(n, m, kind, hh, par):
                    for e in range(2):
                        pe.wait_ge(emptied[2 + e], m + (base1[2 + e] + 1))
                    if kind == 0:
                        for t in range(TT):
                            pe.wait_ge(emptied[4 + t], n + base1[4 + t])
                    heads = [(e, x_, h) for e in range(2) for x_, h in heads_of(kind, e)]
                    if kind < 2:
                        for t in range(TT):
                            for q, (e, x_, h) in enumerate(heads):
                                a = mm(bank[4 + t][:, DH * h:DH * h + DH], PB[:, par, e, S * x_ + P * t:S * x_ + P * t + P],
                                       V[:, hh, 0, DH * h:DH * h + DH], kind == 0 and q == 0, True, skip_group_check=True)
                            if t == 0 and kind == 1:
                                a.then_inc(filled[4], 1)
                            if t == 1:
                                a.then_inc(av_done, 1)
                    else:
                        for e, x_, h in heads:
                            a = mm(bank[5][:, DH * h:DH * h + DH], PB[:, par, e, P * x_:P * x_ + P],
                                   V[:, hh, 1, DH * h:DH * h + DH], False, True, skip_group_check=True)
                        a.then_inc(filled[5], 1)

                def turn_outputs(key, U, i, n, hh):
                    for t in range(TT):
                        pe.wait_ge(emptied[4 + t], n + (base1[4 + t] + 1))
                        k = open_bank(U, (key, f"t{t}"), i)
                        for j in range(4):
                            a = nc.tensor.transpose(bank[k][:, P * j:P * j + P], OG[:, hh, t, P * j:P * j + P], IDN[:, :])
                        a.then_inc(filled[k], 1)

                def output_projection(key, U, i):
                    for t in range(TT):
                        k = U.bank((key, f"t{t}"))
                        if k != U.bank((key, "y")):
                            pe.wait_ge(emptied[k], U.done((key, f"t{t}"), i))
                    k = open_bank(U, (key, "y"), i)
                    for t in range(TT):
                        for j in range(HT0):
                            a = mm(bank[k][:, D * t:D * t + D], OT[:, j // 4, t, j % 4, :], WOR[:, j, :], j == 0, j == HT0 - 1)
                    a.then_inc(filled[k], 1)

                def half(key, U, i, n, b, hh, u, at_least):
                    for k in (6, 7):
                        pe.wait_ge(emptied[k], U.before(key, k, i))
                    if at_least == 2:
                        loads = {0: i + 1, 1: i + 1, 2: i + 2, 3: i + 2, 4: i + 2}
                        loads_b, loads_next = loads[key], loads[key + 1]
                    else:
                        loads_b, loads_next = b // 2 + 1, (b + hh) // 2 + 1
                    b_next, u_next = b + hh, (u + hh) % 2
                    for p in range(3):
                        scores(3 * n + p, p, hh)
                        if p == 1 and at_least >= 1:
                            turn_outputs(key, U, i, n - 1, 1 - hh)
                        if p == 2 and hh == 0 and at_least >= 2:
                            output_projection(key, U, i)
                        if at_least < 15:
                            if p == 0:
                                pe.wait_ge(s_htb[u_next], 16 * loads_next)
                            projections(key, U, i, 1 - hh, u_next, PROJ[p])
                        outputs(n, 3 * n + p, p, hh, (hh + p) % 2)
                        if p < 2:
                            arguments(3 * n + (p + 1), p + 1, hh, u, 32 * loads_b, 16 * (b + 1))
                        elif at_least < 15:
                            arguments(3 * n + 3, 0, 1 - hh, u_next, 32 * loads_next, 16 * (b_next + 1))

                pe.wait_ge(s_wa_hi, 5)
                pe.wait_ge(s_wa_lo, 5)
                pe.wait_ge(s_htb[0], 16)
                for names in PROJ:
                    projections(-1, U_p1[-1], 0, 0, 0, names)
                arguments(0, 0, 0, 0, 32, 16)
                pe.wait_ge(s_wo_n, 1)
                run_halves(pe, half)
                turn_outputs(16, U_p1[16], 0, 15, 1)
                output_projection(16, U_p1[16], 0)
                boundary(1, misc_of("gate_w"), E0)
            if phases >= 2:
                def expert_products(x, u, g):
                    k = g % 2
                    for q in range(2):
                        pe.wait_ge(emptied[2 * q + k], 2 * x + (base2[2 * q + k] + g // 2))
                        w = (FWH, FWL)
                        split_product(bank[2 * q + k][:, :], lambda p_: w[p_][:, u, P * q:P * q + P],
                                      lambda p_: HT[:, p_, GW * g:GW * g + GW]).then_inc(filled[2 * q + k], 1)

                def expert_down(x, u, g):
                    k = g % 2
                    pe.wait_ge(emptied[2 + k], 2 * x + (base2[2 + k] + g // 2 + 1))
                    pe.wait_ge(emptied[4 + k], 2 * x + (base2[4 + k] + g // 2))
                    for t in range(GT):
                        a = mm(bank[4 + k][:, D * t:D * t + D], HB[:, k, P * t:P * t + P], FW[:, u, 2, :], True, True)
                    a.then_inc(filled[4 + k], 1)

                def expert(x, u, at_least):
                    pe.wait_ge(s_fw_hi, x + 1)
                    pe.wait_ge(s_fw_lo, x + 1)
                    for g in range(NG):
                        expert_products(x, u, g)
                        if g:
                            expert_down(x, u, g - 1)
                        elif at_least:
                            expert_down(x - 1, 1 - u, NG - 1)
                pe.wait_ge(s_ht, 2 * NG)
                expert(0, 0, 0)
                with pe.Fori(0, E0 // 2) as i:
                    expert(2 * i + 1, 1, 1)
                    expert(2 * i + 2, 0, 1)
                expert_down(E0, 0, NG - 1)
                boundary(2, None, 0)
            if phases >= 3:
                def project1(key, U, i, v, name):
                    j = int(name[1])
                    k = open_bank(U, (key, name), i)
                    w = (WLH, WLL)
                    if name[0] == "k":
                        for h in range(2):
                            c = P * (2 * j + h)
                            a = split_product(bank[k][:, S * h:S * h + S], lambda p_: w[p_][:, 1, c:c + P],
                                              lambda p_: HTB[:, v, p_, :])
                    else:
                        what = 0 if name[0] == "q" else 2
                        a = split_product(bank[k][:, :], lambda p_: HTB[:, v, p_, P * j:P * j + P],
                                          lambda p_: w[p_][:, what, :])
                    a.then_inc(filled[k], 1)

                def batch(key, U, i, b, u, tail, proj, loads):
                    v = 1 - u
                    if tail:
                        for t in range(TT):
                            open_bank(U, (key, f"kT{t}"), i)
                        for t in range(TT):
                            k = U.bank((key, f"kT{t}"))
                            for j in range(HT1):
                                a = nc.tensor.transpose(bank[k][:, P * j:P * j + P], KE[:, u, j, P * t:P * t + P], IDN[:, :])
                            a.then_inc(filled[k], 1)
                    if proj:
                        pe.wait_ge(s_htb[v], loads)
                        project1(key, U, i, v, "q0")
                        project1(key, U, i, v, "q1")
                    if tail:
                        pe.wait_ge(s_qn, 2 * b + 2)
                        for q in range(2):
                            k = open_bank(U, (key, f"qT{q}"), i)
                            for j in range(2):
                                for t in range(TT):
                                    a = nc.tensor.transpose(bank[k][:, S * j + P * t:S * j + P * t + P],
                                                            QN[:, u, t, P * (2 * q + j):P * (2 * q + j) + P], IDN[:, :])
                            a.then_inc(filled[k], 1)
                    if proj:
                        project1(key, U, i, v, "k0")
                        project1(key, U, i, v, "k1")
                    if tail:
                        for t in range(TT):
                            k = U.bank((key, f"kT{t}"))
                            pe.wait_ge(emptied[k], U.done((key, f"kT{t}"), i))
                        k = open_bank(U, (key, "ctx"), i)
                        for j in range(HT1):
                            for t in range(TT):
                                a = mm(bank[k][:, P * j:P * j + P], VV[:, u, t, P * j:P * j + P],
                                       KT[:, u, t, P * j:P * j + P], t == 0, t == 1)
                        a.then_inc(filled[k], 1)
                    if proj:
                        project1(key, U, i, v, "v0")
                    if tail:
                        c = U.bank((key, "ctx"))
                        pe.wait_ge(emptied[c], U.done((key, "ctx"), i))
                        k = open_bank(U, (key, "m"), i)
                        for j in range(HT1):
                            a = mm(bank[k][:, D * j:D * j + D], CT[:, u, j, :], WO1[:, j, :], True, True)
                        a.then_inc(filled[k], 1)
                    if proj:
                        project1(key, U, i, v, "v1")
                    if tail:
                        for name in ("m", "qT0", "qT1"):
                            c = U.bank((key, name))
                            pe.wait_ge(emptied[c], U.done((key, name), i))
                        k = open_bank(U, (key, "y"), i)
                        for t in range(TT):
                            for j in range(HT1):
                                a = mm(bank[k][:, D * t:D * t + D], QT[:, u, j, P * t:P * t + P], MS[:, u, j, :],
                                       j == 0, j == HT1 - 1)
                        a.then_inc(filled[k], 1)

                pe.wait_ge(s_wl_hi, 1)
                pe.wait_ge(s_wl_lo, 1)
                batch(-1, U_p3[-1], 0, -1, 1, False, True, 16 * 5)
                with pe.Fori(0, 3) as i:
                    batch(0, U_p3["loop"], i, 2 * i, 0, True, True, 16 * i + 16 * 5)
                    batch(1, U_p3["loop"], i, 2 * i + 1, 1, True, True, 16 * i + 16 * 6)
                batch(6, U_p3[6], 0, 6, 0, True, True, 16 * 8)
                batch(7, U_p3[7], 0, 7, 1, True, False, 0)
                boundary(3, misc_of("w_router"), E1)
            if phases >= 4:
                pe.wait_ge(s_comb, 1)
                for g in range(NG):
                    k = open_bank(U_wt, ("wt", g))
                    for t in range(GT):
                        a = mm(bank[k][0:E1, P * t:P * t + P], COMB[:, GT * g + t, 0:E1], IDN[:, :], True, True)
                    a.then_inc(filled[k], 1)
                for g in range(NG):
                    pe.wait_ge(emptied[4 + g], U_wt.done(("wt", g)))
                    k = open_bank(U_wt, ("b2", g))
                    for t in range(GT):
                        a = mm(bank[k][:, D * t:D * t + D], WT[:, GW * g + P * t:GW * g + P * t + P], B2[:, :], True, True)
                    a.then_inc(filled[k], 1)

                def expert4_hidden(e, u, g):
                    w = (WEH, WEL)
                    for f in range(FT):
                        pe.wait_ge(emptied[f], 4 * e + (base4[f] + g))
                        split_product(bank[f][:, :], lambda p_: w[p_][:, u, P * f:P * f + P],
                                      lambda p_: HT[:, p_, GW * g:GW * g + GW]).then_inc(filled[f], 1)

                def expert4_down(e, u, g):
                    k = g % 2
                    pe.wait_ge(emptied[FT - 1], 4 * e + (base4[FT - 1] + g + 1))
                    pe.wait_ge(emptied[4 + k], 2 * e + (base4[4 + k] + g // 2))
                    for t in range(GT):
                        for f in range(FT):
                            a = mm(bank[4 + k][:, D * t:D * t + D], HF[:, k, f, P * t:P * t + P],
                                   WE[:, u, P * (FT + f):P * (FT + f) + P], f == 0, f == FT - 1)
                    a.then_inc(filled[4 + k], 1)

                def expert4(e, u, at_least):
                    pe.wait_ge(s_we_hi, e + 1)
                    pe.wait_ge(s_we_lo, e + 1)
                    for g in range(NG):
                        expert4_hidden(e, u, g)
                        if g:
                            expert4_down(e, u, g - 1)
                        elif at_least:
                            expert4_down(e - 1, 1 - u, NG - 1)
                pe.wait_ge(s_ht, 4 * NG)
                expert4(0, 0, 0)
                with pe.Fori(0, E1 // 2 - 1) as i:
                    expert4(2 * i + 1, 1, 1)
                    expert4(2 * i + 2, 0, 1)
                expert4(E1 - 1, 1, 1)
                expert4_down(E1 - 1, 1, NG - 1)


def lay_out(i):
    t = np.transpose
    f = np.ascontiguousarray

    def rows(w, n):
        return t(w.reshape(n, P, -1), (1, 0, 2))

    small = {
        "c": np.concatenate([t(i["L0_c"]), t(i["L1_c"])], 1),
        "wd": t(i["L0_attn_Wd"]),
        "bd": np.broadcast_to(i["L0_attn_bd"], (P, H0)),
        "norm_w": t(i["L0_attn_norm_w"].reshape(HT0, P)),
        "gate_w": t(i["L0_ffn_gate_w"]),
        "ebias": np.broadcast_to(i["L0_ffn_expert_bias"], (P, E0)),
        "w_router": i["L1_ffn_W_router"],
        "b_router": np.broadcast_to(i["L1_ffn_b_router"], (P, E1)),
        "bo": np.broadcast_to(i["L1_attn_bo"], (P, D)),
    }
    gate = np.concatenate([i["L0_ffn_shared_gate_w"][None], i["L0_ffn_w_gate"]])
    up = np.concatenate([i["L0_ffn_shared_up_w"][None], i["L0_ffn_w_up"]])
    down = np.concatenate([i["L0_ffn_shared_down_w"][None], i["L0_ffn_w_down"]])
    w2 = i["L1_ffn_W2"].reshape(E1, FT, P, D)
    return {
        "x": f(i["L0_attn_x"]),
        "misc": f(np.concatenate([small[n] for n in MISC], 1)),
        "wmod": f(np.stack([i["L0_wmod"], i["L1_wmod"]], 1)),
        "wa": f(np.stack([t(i["L0_attn_" + n]) for n in ("Wq", "Wk", "Wv", "Wg", "Wog")], 1)),
        "woT": f(rows(t(i["L0_attn_Wo"]), HT0)),
        "w_ffn0": f(np.stack([t(gate, (0, 2, 1)), t(up, (0, 2, 1)), t(down, (0, 2, 1))], 2)),
        "w_l1": f(np.stack([i["L1_attn_" + n] for n in ("Wq", "Wk", "Wv")], 1)),
        "wo1": f(rows(i["L1_attn_Wo"], HT1)),
        "w_ffn1": f(np.concatenate([i["L1_ffn_W1"], t(w2, (0, 2, 1, 3)).reshape(E1, P, FT * D),
                                    t(i["L1_ffn_b1"].reshape(E1, FT, P), (0, 2, 1))], 2)),
        "b2": f(i["L1_ffn_b2"]),
    }


def kernel(**inputs):
    import concourse.bacc as bacc
    from concourse.bass_utils import run_bass_kernel_spmd

    arrays = lay_out({n: np.asarray(a) for n, a in inputs.items()})
    nc = bacc.Bacc("TRN2", target_bir_lowering=False, num_devices=1)
    aps = [nc.dram_tensor(n, a.shape, mybir.dt.from_np(a.dtype), kind="ExternalInput").ap() for n, a in arrays.items()]
    out = nc.dram_tensor("out", (B, S, D), F32, kind="ExternalOutput").ap()
    build(nc, *aps, out)
    r = run_bass_kernel_spmd(nc, [arrays], core_ids=[0])
    return r.results[0]["out"]
```

```python
from contextlib import ExitStack

import numpy as np

import concourse.bass as bass
from concourse import mybir
from concourse.alu_op_type import AluOpType as ALU

ACT = mybir.ActivationFunctionType
AX_X = mybir.AxisListType.X
F32 = mybir.dt.float32
F32R = mybir.dt.float32r

P = 128
D = 128
B = 8
S = 256
TT = S // P
NT = B * TT
NG = 4
GT = NT // NG
GW = GT * P

H0, DH = 16, 64
HID0 = H0 * DH
HT0 = HID0 // P
HALF = H0 // 2
E0 = 16
K0 = 8
ROUTE_SCALE = 2.826
H1 = 8
HID1 = H1 * DH
HT1 = HID1 // P
E1 = 8
FT = 4
LN_EPS = 1e-5
RMS_EPS = float(np.finfo(np.float32).eps)
BIG = 3.0e38

MISC = {}
_at = 0
for _name, _n in (("c", 2 * B), ("wd", H0), ("bd", H0), ("norm_w", HT0), ("gate_w", E0), ("ebias", E0),
                  ("w_router", E1), ("b_router", E1), ("bo", D)):
    MISC[_name] = (_at, _at + _n)
    _at += _n
MISC_W = _at


class Banks:

    def __init__(self):
        self.base = [0] * 8

    def phase(self, table, times=1):
        u = Uses(list(self.base), table)
        for k in range(8):
            self.base[k] += u.per[k] * times
        return u


class Uses:
    def __init__(self, base, table):
        self.at, self.base, self.per = {}, base, [0] * 8
        self.marks = {}
        for name, bank in table:
            if bank is None:
                self.marks[name] = list(self.per)
                continue
            self.at[name] = (bank, self.per[bank])
            self.per[bank] += 1

    def before(self, mark, bank, i=0):
        return self.per[bank] * i + (self.base[bank] + self.marks[mark][bank])

    def bank(self, name):
        return self.at[name][0]

    def free(self, name, i=0):
        bank, n = self.at[name]
        return self.per[bank] * i + (self.base[bank] + n)

    def done(self, name, i=0):
        bank, n = self.at[name]
        return self.per[bank] * i + (self.base[bank] + n + 1)


class Chain:

    def __init__(self, sem):
        self.sem, self.base, self.k, self.i, self.per = sem, 0, 0, 0, 0

    def loop(self, i, per):
        self.base, self.k, self.i, self.per = self.base + self.k, 0, i, per

    def end(self, times):
        assert self.k == self.per, (self.k, self.per)
        self.base, self.k, self.i, self.per = self.base + self.per * times, 0, 0, 0

    def __call__(self, eng, ins):
        ins.then_inc(self.sem, 1)
        self.k += 1
        eng.wait_ge(self.sem, self.per * self.i + (self.base + self.k))


def build(nc, x, misc, wmod, wa, woT, w_ffn0, w_l1, wo1, w_ffn1, b2, out, phases=4):
    gate_scratch = nc.dram_tensor("gate_scratch", (2, 2, B, D), F32).ap()
    decay_scratch = nc.dram_tensor("decay_scratch", (2, B, H0, S), F32).ap()
    x_tiles = x.rearrange("b (h p) d -> p (b h) d", p=P)
    out_tiles = out.rearrange("b (h p) d -> p (b h) d", p=P)

    banks = Banks()
    BEFORE = (0, NG, NG + B, 2 * NG + B)

    ctx = ExitStack()
    with ctx:
        def sb(name, shape, dt=F32, stack=ctx):
            return stack.enter_context(nc.sbuf_tensor(name, shape, dt))

        def sem(name):
            return ctx.enter_context(nc.semaphore(name))

        bank = [ctx.enter_context(nc.psum_tensor(f"bank{k}", [P, 512], F32)) for k in range(8)]
        filled = [sem(f"filled{k}") for k in range(8)]
        emptied = [sem(f"emptied{k}") for k in range(8)]

        X = sb("X", [P, NT, D])
        HT = sb("HT", [P, 2, NT * P], F32R)
        HTB = sb("HTB", [P, 2, 2, S], F32R)
        GB = sb("GB", [P, 2, B, D])
        MODT = sb("MODT", [P, 2, 4, B])
        M = sb("M", [P, MISC_W])
        IDN = sb("IDN", [P, P])
        XH = sb("XH", [P, 2, GT, D])
        H32 = sb("H32", [P, 2, GW])
        ST = sb("ST", [P, NT, 6])
        MV = sb("MV", [P, NT, 2])
        RS = sb("RS", [P, NT])
        SC = sb("SC", [P, 2, B])
        MHALF = sb("MHALF", [P, GT])
        BST = sb("BST", [P, 2, TT, 6])
        BMV = sb("BMV", [P, 2, TT, 2])
        BRS = sb("BRS", [P, 2, TT])
        EPS_T = sb("EPS_T", [P, TT])
        SCORE = sb("SCORE", [P, 2, TT, E0])
        CHOICE = sb("CHOICE", [P, 2, TT, E0])
        LEFT = sb("LEFT", [P, 2, TT, E0])
        TOP8 = sb("TOP8", [P, 2, TT, 8])
        TOTAL = sb("TOTAL", [P, 2, TT])
        PAD = sb("PAD", [P, 1])
        COMB = sb("COMB", [P, NT, E0 + 1])
        B2 = sb("B2", [E1, D])
        FW = sb("FW", [P, 2, 3, P])
        FWH = sb("FWH", [P, 2, 2 * P], F32R)
        FWL = sb("FWL", [P, 2, 2 * P], F32R)

        def misc_of(name):
            a, b = MISC[name]
            return M[:, a:b]

        s_misc = sem("s_misc")
        s_mod = sem("s_mod")
        s_x = [sem(f"s_x{g}") for g in range(NG)]
        s_silu = sem("s_silu")
        s_idn = sem("s_idn")
        s_tri = sem("s_tri")
        s_rows_in = sem("s_rows_in")
        s_rows = sem("s_rows")
        s_gates = sem("s_gates")
        s_gates_out = sem("s_gates_out")
        s_gb = sem("s_gb")
        s_wa_raw = [sem(f"s_wa_raw{k}") for k in range(5)]
        s_wa_hi = sem("s_wa_hi")
        s_wa_lo = sem("s_wa_lo")
        s_wa_lo_v = sem("s_wa_lo_v")
        s_wo = sem("s_wo")
        s_wo_n = sem("s_wo_n")
        s_var = sem("s_var")
        s_rstd = sem("s_rstd")
        s_rms = sem("s_rms")
        s_pchain = sem("s_pchain")
        s_xh = sem("s_xh")
        s_ht = sem("s_ht")
        s_chain = sem("s_chain")
        s_nabs = sem("s_nabs")
        s_exp = sem("s_exp")
        s_log = sem("s_log")
        s_ld = sem("s_ld")
        s_nout = sem("s_nout")
        s_htb = [sem(f"s_htb{k}") for k in range(2)]
        s_lg = [sem(f"s_lg{k}") for k in range(2)]
        s_rg = [sem(f"s_rg{k}") for k in range(2)]
        mask_done = sem("mask_done")
        av_done = sem("av_done")
        sq_done = sem("sq_done")
        s_hsum = sem("s_hsum")
        s_ssq = sem("s_ssq")
        x_done = sem("x_done")
        s_logits = sem("s_logits")
        s_rexp = sem("s_rexp")
        s_comb = sem("s_comb")
        s_fw = [sem(f"s_fw{k}") for k in range(2)]
        s_fw_hi = sem("s_fw_hi")
        s_fw_lo = sem("s_fw_lo")
        s_wl_raw = sem("s_wl_raw")
        s_wl_hi = sem("s_wl_hi")
        s_wl_lo = sem("s_wl_lo")
        s_ct0 = sem("s_ct0")
        s_qe = sem("s_qe")
        s_gated = sem("s_gated")
        s_qs = sem("s_qs")
        s_qn = sem("s_qn")
        s_kmax = sem("s_kmax")
        s_we = [sem(f"s_we{k}") for k in range(2)]
        s_we_hi = sem("s_we_hi")
        s_we_lo = sem("s_we_lo")
        s_out = sem("s_out")
        link = Chain(s_chain)
        link_pool = Chain(s_pchain)

        U_mod = banks.phase([("modT", 0), ("gates", 5)])

        def boundary_table(routed=True):
            t = []
            for g in range(NG + 1):
                if g < NG:
                    t.append((("tr", g), g % 2))
                if g and routed:
                    t.append((("rt", g - 1), 2 + (g - 1) % 2))
            return t

        U_b = [None] * 4
        U_b[0] = banks.phase(boundary_table())
        U_n = banks.phase([("n", 4)])

        HALVES = 2 * B
        LOOPED = 12
        PROJ = (("q0", "g0", "k0", "q1"), ("g1", "k1", "v0"), ("o0", "v1", "o1"))
        turn = [0]

        def other(key, name):
            turn[0] += 1
            return ((key, name), 6 + turn[0] % 2)

        def half_table(key, y, proj, norm=False):
            t = [(key, None)]
            for p in range(3):
                if p >= 1 and y:
                    t.append(other(key, ("ss", "y")[p - 1]))
                if proj:
                    t += [other(key, n) for n in PROJ[p]]
                if norm and p >= 1:
                    t.append(other(key, ("tr", "rt")[p - 1]))
            return t

        base1 = list(banks.base)
        U_p1 = {-1: banks.phase([other(-1, n) for step in PROJ for n in step])}
        U_p1[0] = banks.phase(half_table(0, False, True))
        U_p1[1] = banks.phase(half_table(1, False, True))
        t = [use for r in range(4) for use in half_table(r, r % 2 == 0, True, r % 2 == 1)]
        assert sum(k is not None for _, k in t) % 2 == 0
        U_p1["loop"] = banks.phase(t, LOOPED // 4)
        U_p1[14] = banks.phase(half_table(14, True, True))
        U_p1[15] = banks.phase(half_table(15, False, False, True))
        U_p1[16] = banks.phase([other(16, name) for name in ("y", "ss", "tr", "rt")])
        for k in range(4):
            banks.base[k] += 3 * HALVES
        for k in (4, 5):
            banks.base[k] += HALVES

        base2 = list(banks.base)
        if phases >= 2:
            for k in range(6):
                banks.base[k] += (E0 + 1) * NG // 2
        U_b[2] = banks.phase(boundary_table(False))

        def batch_table(key, u, proj, norm):
            here, there = 4 * u, 4 * (1 - u)
            t = [("kT0", here + 2), ("kT1", here + 3)]
            t += [("q0", there), ("q1", there + 1)] if proj else []
            t += [("qT0", here), ("qT1", here + 1)]
            t += [("k0", there + 2), ("k1", there + 3)] if proj else []
            t += [("ctx", here + 2)]
            t += [("v0", there)] if proj else []
            t += [("tr", here + 1)] if norm else []
            t += [("m", here + 3)]
            t += [("v1", there + 1)] if proj else []
            t += [("rt", here + 2)] if norm else []
            t += [("y", here)]
            return [((key, name), k) for name, k in t]

        U_p3 = {-1: banks.phase([((-1, "q0"), 0), ((-1, "q1"), 1), ((-1, "k0"), 2), ((-1, "k1"), 3),
                                 ((-1, "v0"), 0), ((-1, "v1"), 1)]),
                0: banks.phase(batch_table(0, 0, True, False)),
                "loop": banks.phase(batch_table(1, 1, True, True) + batch_table(2, 0, True, True), 3),
                7: banks.phase(batch_table(7, 1, False, True)),
                8: banks.phase([((8, "tr"), 6), ((8, "rt"), 7)])}
        U_wt = banks.phase([(("wt", g), 6 + g % 2) for g in range(NG)] + [(("b2", g), 6 + g % 2) for g in range(NG)])
        base4 = list(banks.base)

        with ExitStack() as stack1:
            def s1(name, shape, dt=F32):
                return sb(name, shape, dt, stack1)

            TRI = s1("TRI", [P, 2 * P])
            WAH = s1("WAH", [P, 5, HID0], F32R)
            WAL = s1("WAL", [P, 5, HID0], F32R)
            WOR = s1("WOR", [P, HT0, D])
            Z = s1("Z", [P, TT, B, H0])
            ZA = s1("ZA", [P, TT, B, H0])
            GS = s1("GS", [B, 4, D])
            GA = s1("GA", [B, 4, D])
            LG = s1("LG", [96, 2, S], F32R)
            RG = s1("RG", [96, 2, HALF, S], F32R)
            Q = s1("Q", [P, 2, 4, S])
            KG = s1("KG", [P, 2, 4, S])
            TG = s1("TG", [P, 2, 2 * S])
            V = s1("V", [P, 2, TT, HALF * DH])
            TO = s1("TO", [P, 2, 4, S])
            DB = s1("DB", [P, 2, 2, 512])
            PB = s1("PB", [P, 2, 2, 512])
            SQ = s1("SQ", [P, 2, 512])
            HS = s1("HS", [P, 2, 512])
            BS = s1("BS", [P, 512])
            SSQ = s1("SSQ", [P, S])
            SR = s1("SR", [P, 2, TT])
            RMS_B = s1("RMS_B", [P, 1])
            ONE = s1("ONE", [P, 1])
            OT = s1("OT", [P, 2, 4, S])
            TMP = s1("TMP", [P, TT, D])

        def s2(name, shape, dt=F32):
            return sb(name, shape, dt)

        ACC = s2("ACC", [P, NT, D])
        SEL = s2("SEL", [P, NT, E0])
        M8 = s2("M8", [P, NT, 8])
        REP = s2("REP", [P, NT, E0])
        SCO = s2("SCO", [P, NT, E0])
        SUM = s2("SUM", [P, NT])
        VAL = s2("VAL", [P, NT, E1 + 6])
        SIL = s2("SIL", [P, 2, GW])
        HB = s2("HB", [P, 2, GW])
        WT = s2("WT", [E1, NT * P])
        WE = s2("WE", [P, 2, 2 * FT * P + FT])
        WEH = s2("WEH", [P, 2, FT * P], F32R)
        WEL = s2("WEL", [P, 2, FT * P], F32R)
        WLR = s2("WLR", [P, 3, HID1])
        WLH = s2("WLH", [P, 3, HID1], F32R)
        WLL = s2("WLL", [P, 3, HID1], F32R)
        WO1 = s2("WO1", [P, HT1, D])
        QM = s2("QM", [P, 2, TT, H1])
        QS = s2("QS", [P, 2, TT, H1])
        QE = s2("QE", [P, 2, TT, HID1])
        QN = s2("QN", [P, 2, TT, HID1])
        KM = s2("KM", [P, 2, HT1])
        KS = s2("KS", [P, 2, HT1])
        RK = s2("RK", [P, 2, HT1])
        KE = s2("KE", [P, 2, HT1, S])
        KT = s2("KT", [P, 2, TT, HID1])
        VV = s2("VV", [P, 2, TT, HID1])
        QT = s2("QT", [P, 2, HT1, S])
        CT = s2("CT", [P, 2, HT1, P])
        MS = s2("MS", [P, 2, HT1, D])
        YT = s2("YT", [P, 2, TT, D])
        HF = s2("HF", [P, 2, FT, GW])

        WRAW = [T[:, k, :, :].rearrange("p m t -> p (m t)") for T in (Q, KG) for k in range(2)]
        WRAW.append(TG[:, :, :].rearrange("p j n -> p (j n)"))
        WM = OT[:, :, :, :].rearrange("p a t n -> p (a t n)")[:, 0:12 * D].rearrange("p (l n) -> p l n", l=2)
        N_HI, N_LO = PB[:, 0, 0, 0:S], PB[:, 0, 1, 0:S]

        def run_halves(eng, half):
            for n in (0, 1):
                half(n, U_p1[n], 0, n, 0, n, 0, n)
            with eng.Fori(0, LOOPED // 4) as i:
                if eng is nc.gpsimd:
                    link_pool.loop(i, 4)
                if eng is nc.vector:
                    link.loop(i, 22)
                for r in range(4):
                    half(r, U_p1["loop"], i, 4 * i + (2 + r), 2 * i + (1 + r // 2), r % 2, (1 + r // 2) % 2, 2)
                if eng is nc.gpsimd:
                    link_pool.end(LOOPED // 4)
                if eng is nc.vector:
                    link.end(LOOPED // 4)
            for n in (14, 15):
                half(n, U_p1[n], 0, n, 7, n % 2, 1, n)

        def run_batches(eng, batch):
            batch(-1, U_p3[-1], 0, -1, 1, False, True, False)
            batch(0, U_p3[0], 0, 0, 0, True, True, False)
            with eng.Fori(0, 3) as i:
                if eng is nc.gpsimd:
                    link_pool.loop(i, 2)
                if eng is nc.vector:
                    link.loop(i, 20)
                batch(1, U_p3["loop"], i, 2 * i + 1, 1, True, True, True)
                batch(2, U_p3["loop"], i, 2 * i + 2, 0, True, True, True)
                if eng is nc.gpsimd:
                    link_pool.end(3)
                if eng is nc.vector:
                    link.end(3)
            batch(7, U_p3[7], 0, 7, 1, True, False, True)

        def heads_of(kind, par):
            if kind < 2:
                return [(m, 4 * kind + 2 * m + par) for m in range(2)]
            return [(m, 2 * m + par) for m in range(4)]

        block = ctx.enter_context(nc.Block())

        @block.sync
        def _(sp):
            sp.dma_start(M[:, :], misc).then_inc(s_misc, 16)
            sp.dma_start(X[:, 0:GT, :], x_tiles[:, 0:GT, :]).then_inc(s_x[0], 16)
            sp.dma_start(WM, wmod).then_inc(s_mod, 16)
            for g in range(1, NG):
                sp.dma_start(X[:, GT * g:GT * g + GT, :], x_tiles[:, GT * g:GT * g + GT, :]).then_inc(s_x[g], 16)
            for c in range(5):
                sp.dma_start(WRAW[c], wa[:, c, :]).then_inc(s_wa_raw[c], 16)
            sp.dma_start(WOR[:, :, :], woT).then_inc(s_wo, 16)
            sp.dma_start(B2[:, :], b2).then_inc(s_wo, 16)
            for k in range(2):
                sp.dma_start(FW[:, k, :, :], w_ffn0[k]).then_inc(s_fw[k], 16)

            def load_htb(b, u):
                sp.dma_start(HTB[:, u, :, :].bitcast(F32), HT[:, :, bass.ds(b * S, S)].bitcast(F32)).then_inc(s_htb[u], 16)

            def load_lg(b, u):
                for part in range(2):
                    sp.dma_start(LG[32 + 32 * part:32 + 32 * part + H0, u, :].bitcast(F32),
                                 decay_scratch[part, bass.ds(b, 1), :, :].rearrange("o h t -> (o h) t")).then_inc(s_lg[u], 16)

            def load_rg(b, hh):
                sp.dma_start(RG[0:2, hh, :, :].bitcast(F32),
                             decay_scratch[:, bass.ds(b, 1), hh * HALF:(hh + 1) * HALF, :].rearrange("c o h t -> c (o h) t")).then_inc(s_rg[hh], 16)

            if phases >= 1:
                sp.wait_ge(s_ht, 1)
                load_htb(0, 0)
                load_htb(1, 1)
                sp.wait_ge(emptied[4], U_n.done("n"))
                for part, src in enumerate((N_HI, N_LO)):
                    sp.dma_start(decay_scratch[part].rearrange("b h t -> (b h) t"), src).then_inc(s_nout, 16)
                sp.wait_ge(s_nout, 32)
                sp.wait_ge(s_rows, 1)
                load_lg(0, 0)
                load_rg(0, 0)
                load_rg(0, 1)
                load_lg(1, 1)
                sp.wait_ge(s_gates, 1)
                sp.dma_start(gate_scratch.rearrange("l a b d -> b (l a) d"), GS[:, :, :]).then_inc(s_gates_out, 16)
                sp.wait_ge(s_gates_out, 16)
                flat_gb = GB[:, :, :, :].rearrange("p a b d -> p (a b d)")
                sp.dma_start(flat_gb, gate_scratch[0].rearrange("a b d -> (a b d)").partition_broadcast(P)).then_inc(s_gb, 16)

                def half(key, U, i, n, b, hh, u, at_least):
                    if hh == 0 and 1 <= at_least < 14:
                        sp.wait_ge(filled[3], 3 * n + (base1[3] + 1))
                        load_htb(b + 1, 1 - u)
                        load_lg(b + 1, 1 - u)
                    if at_least < 14:
                        sp.wait_ge(filled[1], 3 * n + (base1[1] + 3))
                        load_rg(b + 1, hh)
                run_halves(sp, half)
            if phases >= 2:
                def reload(x, u):
                    sp.wait_ge(s_fw_lo, x + 1)
                    sp.wait_ge(filled[5], 2 * x + (base2[5] + 2))
                    sp.dma_start(FW[:, u, :, :], w_ffn0[bass.ds(x + 2, 1)].rearrange("o p k n -> p (o k) n")).then_inc(s_fw[u], 16)
                sp.wait_ge(x_done, B)
                sp.dma_start(WLR[:, :, :], w_l1).then_inc(s_wl_raw, 16)
                sp.dma_start(WO1[:, :, :], wo1).then_inc(s_wl_raw, 16)
                reload(0, 0)
                with sp.Fori(0, E0 // 2 - 1) as i:
                    reload(2 * i + 1, 1)
                    reload(2 * i + 2, 0)
            if phases >= 3:
                sp.wait_ge(x_done, B + NG)
                sp.dma_start(flat_gb, gate_scratch[1].rearrange("a b d -> (a b d)").partition_broadcast(P)).then_inc(s_gb, 16)
                sp.wait_ge(s_ht, BEFORE[2] + 1)
                load_htb(0, 0)
                load_htb(1, 1)
                for k in range(2):
                    sp.dma_start(WE[:, k, :], w_ffn1[k]).then_inc(s_we[k], 16)
                def batch(key, U, i, b, v):
                    sp.wait_ge(filled[U.bank((key, "v1"))], U.done((key, "v1"), i))
                    load_htb(b + 3, v)
                batch(-1, U_p3[-1], 0, -1, 0)
                batch(0, U_p3[0], 0, 0, 1)
                with sp.Fori(0, 2) as i:
                    batch(1, U_p3["loop"], i, 2 * i + 1, 0)
                    batch(2, U_p3["loop"], i, 2 * i + 2, 1)
            if phases >= 4:
                def reload4(e, u):
                    sp.wait_ge(s_we_lo, e + 1)
                    sp.wait_ge(filled[5], 2 * e + (base4[5] + 2))
                    sp.dma_start(WE[:, u, :], w_ffn1[bass.ds(e + 2, 1)].rearrange("o p n -> p (o n)")).then_inc(s_we[u], 16)
                with sp.Fori(0, E1 // 2 - 1) as i:
                    reload4(2 * i, 0)
                    reload4(2 * i + 1, 1)
            before = {0: 0, 1: 0, 2: B, 3: B + NG, 4: 2 * B + NG}[phases]
            for g in range(NG):
                if phases in (2, 4):
                    sp.wait_ge(x_done, before + g + 1)
                elif phases:
                    sp.wait_ge(x_done, before + 2 * (g + 1))
                sp.dma_start(out_tiles[:, GT * g:GT * g + GT, :], X[:, GT * g:GT * g + GT, :]).then_inc(s_out, 16)
            sp.wait_ge(s_out, 16 * NG)

        @block.gpsimd
        def _(pool):
            nc.gpsimd.memset(MHALF[:, :], -0.5)
            nc.gpsimd.memset(IDN[:, :], 0.0).then_inc(s_idn, 1)
            pool.wait_ge(s_idn, 1)
            nc.gpsimd.affine_select(out=IDN[:, :], in_=IDN[:, :], compare_op=ALU.not_equal, fill=1.0, base=0,
                                    pattern=[[-1, P]], channel_multiplier=1).then_inc(s_idn, 1)
            nc.gpsimd.memset(TRI[:, :], 1.0).then_inc(s_tri, 1)
            pool.wait_ge(s_tri, 1)
            nc.gpsimd.affine_select(out=TRI[:, 0:P], in_=TRI[:, 0:P], compare_op=ALU.is_ge, fill=0.0, base=0,
                                    pattern=[[1, P]], channel_multiplier=-1).then_inc(s_tri, 1)
            nc.gpsimd.memset(EPS_T[:, :], LN_EPS)
            nc.gpsimd.memset(RMS_B[:, :], 4.0 * RMS_EPS)
            nc.gpsimd.memset(ONE[:, :], 1.0)
            nc.gpsimd.memset(LG[:, :, :].bitcast(F32), 0.0)
            nc.gpsimd.memset(RG[:, :, :, :].bitcast(F32), 0.0).then_inc(s_rows_in, 1)
            pool.wait_ge(s_rows_in, 1)
            def heads_of_rows(k, hh):
                v = RG[32 + 32 * k:32 + 32 * k + H0, hh, :, :]
                link_pool(pool, nc.gpsimd.affine_select(
                    out=v, in_=v.bitcast(F32), compare_op=ALU.not_equal, fill=1.0, base=-hh * HALF,
                    pattern=[[-1, HALF], [0, S]], channel_multiplier=1))

            def deviations(k, between=(), groups=range(NG)):
                for g in groups:
                    pool.wait_ge(s_var, BEFORE[k] + g + 1)
                    r = RS[:, GT * g:GT * g + GT]
                    link_pool(pool, nc.gpsimd.tensor_scalar(r, MV[:, GT * g:GT * g + GT, 1], LN_EPS, None, ALU.add))
                    nc.gpsimd.tensor_tensor(r, r, MHALF[:, 0:GT], ALU.pow).then_inc(s_rstd, 1)
                    if g < len(between):
                        pool.wait_ge(s_rstd, BEFORE[k] + g + 1)
                        heads_of_rows(*between[g])
            deviations(0, [(k, hh) for k in range(2) for hh in range(2)])
            nc.gpsimd.memset(LG[0:2, :, :].bitcast(F32), -1.0).then_inc(s_rows, 1)
            for c in range(2):
                pool.wait_ge(s_wa_hi, c + 1)
                nc.gpsimd.tensor_tensor(WAL[:, c, :], WRAW[c], WAH[:, c, :].bitcast(F32), ALU.subtract).then_inc(s_wa_lo, 1)
            if phases >= 1:
                def low(x, u):
                    pool.wait_ge(s_fw_hi, x + 1)
                    nc.gpsimd.tensor_tensor(FWL[:, u, :], FW[:, u, 0:2, :].rearrange("p k n -> p (k n)"),
                                            FWH[:, u, :].bitcast(F32), ALU.subtract).then_inc(s_fw_lo, 1)
                def mask(m, par, kind):
                    for e in range(2):
                        pool.wait_ge(emptied[e], m + (base1[e] + 1))
                    if kind < 2:
                        v = DB[:, par, :, :].rearrange("p e (m t) -> p e m t", t=S)[:, :, :, 0:P]
                        pattern = [[0, 2], [0, 2], [1, P - 1]]
                    else:
                        v = DB[:, par, :, :].rearrange("p e (m t) -> p e m t", t=P)
                        pattern = [[0, 2], [0, 4], [1, P - 1]]
                    first, rest = v[:, :, :, 0], v[:, :, :, 1:P]
                    unit = IDN[:, 0:1].unsqueeze(2).to_broadcast(list(first.shape))
                    nc.gpsimd.tensor_tensor(first, unit, unit, ALU.mult).then_inc(mask_done, 1)
                    nc.gpsimd.affine_select(out=rest, in_=rest, compare_op=ALU.is_ge, fill=0.0, base=1, pattern=pattern,
                                            channel_multiplier=-1).then_inc(mask_done, 1)

                def sum_squares(n, hh):
                    pool.wait_ge(sq_done, 2 * n + 2)
                    nc.gpsimd.tensor_tensor(HS[:, hh, :], SQ[:, 0, :], SQ[:, 1, :], ALU.add).then_inc(s_hsum, 1)
                    if hh == 1:
                        pool.wait_ge(s_hsum, n + 1)
                        link_pool(pool, nc.gpsimd.tensor_tensor(BS[:, :], HS[:, 0, :], HS[:, 1, :], ALU.add))
                        nc.gpsimd.tensor_tensor(SSQ[:, :], BS[:, 0:S], BS[:, S:2 * S], ALU.add).then_inc(s_ssq, 1)

                def root_mean_squares(key, U, i, u):
                    k = U.bank((key, "ss"))
                    pool.wait_ge(emptied[k], U.done((key, "ss"), i))
                    nc.gpsimd.tensor_tensor(SR[:, u, :], SR[:, u, :], MHALF[:, 0:TT], ALU.pow).then_inc(s_rms, 1)

                def batch_deviations(k, c, v):
                    pool.wait_ge(s_var, c + (BEFORE[k] + 1))
                    link_pool(pool, nc.gpsimd.tensor_tensor(BRS[:, v, :], BMV[:, v, :, 1], EPS_T[:, :], ALU.add))
                    nc.gpsimd.tensor_tensor(BRS[:, v, :], BRS[:, v, :], MHALF[:, 0:TT], ALU.pow).then_inc(s_rstd, 1)

                def half(key, U, i, n, b, hh, u, at_least):
                    for p in range(3):
                        mask(3 * n + p, (hh + p) % 2, p)
                        if p == 0 and at_least >= 1:
                            sum_squares(n - 1, 1 - hh)
                        if p == 1 and hh == 0 and at_least >= 2:
                            root_mean_squares(key, U, i, 1 - u)
                        if p == 0 and hh == 1 and at_least >= 2:
                            batch_deviations(1, b - 1, 1 - u)
                low(0, 0)
                run_halves(pool, half)
                sum_squares(15, 1)
                root_mean_squares(16, U_p1[16], 0, 1)
                batch_deviations(1, 7, 1)
            if phases >= 2:
                low(1, 1)
                pool.wait_ge(x_done, B)
                nc.gpsimd.memset(CT[:, :, :, :], 0.0).then_inc(s_ct0, 1)
                pool.wait_ge(s_wl_hi, 1)
                nc.gpsimd.tensor_tensor(WLL[:, :, :], WLR[:, :, :], WLH[:, :, :].bitcast(F32), ALU.subtract).then_inc(s_wl_lo, 1)
                with pool.Fori(1, E0 // 2) as i:
                    low(2 * i, 0)
                    low(2 * i + 1, 1)
                low(E0, 0)

                def times_gate(g, ready, value):
                    pool.wait_ge(ready, value)
                    for h in range(2):
                        v = ACC[:, GT * g + TT * h:GT * g + TT * h + TT, :]
                        gb = GB[:, 1, 2 * g + h, :].unsqueeze(1).to_broadcast([P, TT, D])
                        a = nc.gpsimd.tensor_tensor(v, v, gb, ALU.mult)
                    a.then_inc(s_gated, 1)
                for g in range(NG):
                    times_gate(g, emptied[4 + g % 2], base2[4 + g % 2] + 2 * E0 + g // 2 + 1)
                def group_low(q):
                    tr = U_b[2].bank(("tr", q))
                    pool.wait_ge(emptied[tr], U_b[2].done(("tr", q)))
                    h = slice(GW * q, GW * q + GW)
                    nc.gpsimd.tensor_tensor(HT[:, 1, h], H32[:, q % 2, :], HT[:, 0, h].bitcast(F32),
                                            ALU.subtract).then_inc(s_ht, 1)
                deviations(2, groups=(0, 1, 2))
                group_low(0)
                deviations(2, groups=(3,))
                for q in range(1, NG):
                    group_low(q)
            if phases >= 3:
                def batch(key, U, i, b, u, tail, proj, norm):
                    if norm:
                        batch_deviations(3, b - 1, 1 - u)
                    if proj:
                        v = 1 - u
                        for t in range(TT):
                            pool.wait_ge(s_qs, 2 * b + (t + 3))
                            nc.gpsimd.tensor_tensor(QN[:, v, t, :].rearrange("p (h d) -> p h d", d=DH),
                                                    QE[:, v, t, :].rearrange("p (h d) -> p h d", d=DH),
                                                    QS[:, v, t, :].unsqueeze(2).to_broadcast([P, H1, DH]),
                                                    ALU.mult).then_inc(s_qn, 1)
                run_batches(pool, batch)
            if phases >= 4:
                def low4(e, u):
                    pool.wait_ge(s_we_hi, e + 1)
                    nc.gpsimd.tensor_tensor(WEL[:, u, :], WE[:, u, 0:FT * P], WEH[:, u, :].bitcast(F32),
                                            ALU.subtract).then_inc(s_we_lo, 1)
                low4(0, 0)
                batch_deviations(3, 7, 1)
                low4(1, 1)
                with pool.Fori(1, E1 // 2) as i:
                    low4(2 * i, 0)
                    low4(2 * i + 1, 1)
                for g in range(NG):
                    times_gate(g, emptied[4 + g % 2], base4[4 + g % 2] + 2 * (E1 - 1) + g // 2 + 1)

        @block.scalar
        def _(act):
            def act_boundary(k, between=None):
                l, ab = k // 2, k % 2
                U = U_b[k]
                for g in range(NG):
                    act.wait_ge(filled[U.bank(("tr", g))], U.done(("tr", g)))
                    if k == 2 and g >= 2:
                        act.wait_ge(s_ht, BEFORE[k] + g - 1)
                    for h in range(2):
                        b = 2 * g + h
                        for out_ in (H32[:, g % 2, S * h:S * h + S], HT[:, 0, S * b:S * b + S]):
                            a = nc.scalar.activation(out_, bank[U.bank(("tr", g))][:, S * h:S * h + S], ACT.Identity,
                                                     scale=MODT[:, l, 2 * ab + 1, b:b + 1], bias=MODT[:, l, 2 * ab, b:b + 1])
                    a.then_inc(emptied[U.bank(("tr", g))], 1)
                    if between:
                        between(g)

            act.wait_ge(s_misc, 16)
            nc.scalar.activation(SC[:, :, :].rearrange("p l b -> p (l b)"), misc_of("c"), ACT.Silu).then_inc(s_silu, 1)
            act.wait_ge(emptied[0], U_mod.done("modT"))

            def wa_high(c):
                act.wait_ge(s_wa_raw[c], 16)
                nc.scalar.activation(WAH[:, c, :], WRAW[c], ACT.Copy).then_inc(s_wa_hi, 1)
            act_boundary(0, wa_high)
            wa_high(4)
            act.wait_ge(s_nabs, 1)
            za = ZA[:, :, :, :].rearrange("p c b h -> p (c b h)")
            nc.scalar.activation(za, za, ACT.Exp).then_inc(s_exp, 1)
            act.wait_ge(s_exp, 1)
            nc.scalar.activation(za, za, ACT.Ln, bias=1.0).then_inc(s_log, 1)

            def high(x, u, loads):
                act.wait_ge(s_fw[u], loads)
                nc.scalar.activation(FWH[:, u, :], FW[:, u, 0:2, :].rearrange("p k n -> p (k n)"), ACT.Copy).then_inc(s_fw_hi, 1)

            if phases >= 1:
                def project(key, U, i, hh, name, out_, func, scale):
                    k = U.bank((key, name))
                    act.wait_ge(filled[k], U.done((key, name), i))
                    nc.scalar.activation(out_, bank[k][:, :], func, scale=scale).then_inc(emptied[k], 1)

                def projections(key, U, i, hh, names):
                    for name in names:
                        j = int(name[1])
                        if name[0] == "q":
                            project(key, U, i, hh, name, Q[:, hh, 2 * j:2 * j + 2, :].rearrange("p m t -> p (m t)"),
                                    ACT.Copy, 0.5)
                        elif name[0] == "g":
                            project(key, U, i, hh, name, TG[:, j, :], ACT.Tanh, 0.5)
                        elif name[0] == "o":
                            project(key, U, i, hh, name, TO[:, hh, 2 * j:2 * j + 2, :].rearrange("p m t -> p (m t)"),
                                    ACT.Tanh, 0.5)

                def decays(m, par, at_least):
                    if at_least >= 2:
                        for e in range(2):
                            act.wait_ge(emptied[2 + e], m + (base1[2 + e] - 1))
                    for e in range(2):
                        act.wait_ge(filled[e], m + (base1[e] + 1))
                        nc.scalar.activation(DB[:, par, e, :], bank[e][:, :], ACT.Exp).then_inc(emptied[e], 1)

                def squares(n, at_least):
                    if at_least >= 1:
                        act.wait_ge(s_hsum, n)
                    for k in range(2):
                        act.wait_ge(filled[4 + k], n + (base1[4 + k] + 1))
                        nc.scalar.activation(SQ[:, k, :], bank[4 + k][:, :], ACT.Square).then_inc(sq_done, 1)

                def mean_squares(key, U, i, u):
                    k = U.bank((key, "ss"))
                    act.wait_ge(filled[k], U.done((key, "ss"), i))
                    nc.scalar.activation(SR[:, u, :], bank[k][:, 0:TT], ACT.Identity, scale=4.0 / HID0,
                                         bias=RMS_B[:, :]).then_inc(emptied[k], 1)

                def modulate(l, key, U, i, c, v):
                    k = U.bank((key, "tr"))
                    act.wait_ge(filled[k], U.done((key, "tr"), i))
                    for out_ in (H32[:, v, 0:S], HT[:, 0, bass.ds(S * c, S)]):
                        a = nc.scalar.activation(out_, bank[k][:, 0:S], ACT.Identity,
                                                 scale=MODT[:, l, 3, bass.ds(c, 1)], bias=MODT[:, l, 2, bass.ds(c, 1)])
                    a.then_inc(emptied[k], 1)

                def router_exp(key, U, i, v):
                    k = U.bank((key, "rt"))
                    act.wait_ge(filled[k], U.done((key, "rt"), i))
                    nc.scalar.activation(LEFT[:, v, :, :].rearrange("p t e -> p (t e)"), bank[k][:, 0:TT * E0], ACT.Exp,
                                         scale=-1.0).then_inc(emptied[k], 1)

                def half(key, U, i, n, b, hh, u, at_least):
                    norm = hh == 1 and at_least >= 2
                    for p in range(3):
                        if at_least < 15 or p < 2:
                            decays(3 * n + (p + 1), (hh + p + 1) % 2, 3 * at_least + p + 1)
                        if p == 1 and hh == 0 and at_least >= 2:
                            mean_squares(key, U, i, 1 - u)
                        if at_least < 15:
                            projections(key, U, i, 1 - hh, PROJ[p])
                        if norm and p == 1:
                            modulate(0, key, U, i, b - 1, 1 - u)
                        if norm and p == 2:
                            router_exp(key, U, i, 1 - u)
                    squares(n, at_least)
                for names in PROJ:
                    projections(-1, U_p1[-1], 0, 0, names)
                decays(0, 0, 0)
                high(0, 0, 16)
                run_halves(act, half)
                mean_squares(16, U_p1[16], 0, 1)
                modulate(0, 16, U_p1[16], 0, 7, 1)
                router_exp(16, U_p1[16], 0, 1)
            if phases >= 2:
                def gate_step(x, g, first=False):
                    k = g % 2
                    act.wait_ge(filled[k], 2 * x + (base2[k] + g // 2 + 1))
                    if not (first and g < 2):
                        act.wait_ge(emptied[2 + k], 2 * x + (base2[2 + k] + g // 2))
                    nc.scalar.activation(SIL[:, k, :], bank[k][:, :], ACT.Silu).then_inc(emptied[k], 1)

                def expert(x, u, loads, at_least):
                    for g in range(NG):
                        gate_step(x, g, at_least == 0)
                        if g == 2 and at_least < E0:
                            high(x + 1, 1 - u, loads)

                expert(0, 0, 16, 0)
                act.wait_ge(s_wl_raw, 32)
                nc.scalar.activation(WLH[:, :, :], WLR[:, :, :], ACT.Copy).then_inc(s_wl_hi, 1)
                with act.Fori(0, E0 // 2 - 1) as i:
                    expert(2 * i + 1, 1, 16 * i + 32, 1)
                    expert(2 * i + 2, 0, 16 * i + 32, 1)
                expert(E0 - 1, 1, 16 * (E0 // 2 + 1), E0 - 1)
                expert(E0, 0, 0, E0)
                act_boundary(2)
            if phases >= 3:
                def batch(key, U, i, b, u, tail, proj, norm):
                    def copy_out(name, out_):
                        k = U.bank((key, name))
                        act.wait_ge(filled[k], U.done((key, name), i))
                        nc.scalar.activation(out_, bank[k][:, :], ACT.Copy).then_inc(emptied[k], 1)

                    v = 1 - u
                    if tail:
                        for t in range(TT):
                            copy_out(f"kT{t}", KT[:, u, t, :])
                    if proj:
                        for t in range(TT):
                            k = U.bank((key, f"q{t}"))
                            act.wait_ge(emptied[k], U.done((key, f"q{t}"), i))
                            nc.scalar.activation(QE[:, v, t, :], QE[:, v, t, :], ACT.Exp).then_inc(s_qe, 1)
                    if tail:
                        for t in range(2):
                            copy_out(f"qT{t}", QT[:, u, 2 * t:2 * t + 2, :].rearrange("p j t -> p (j t)"))
                    for j in range(2):
                        if proj:
                            k = U.bank((key, f"k{j}"))
                            act.wait_ge(s_kmax, 2 * b + (3 + j))
                            for h in range(2):
                                a = nc.scalar.activation(KE[:, v, 2 * j + h, :], bank[k][:, S * h:S * h + S], ACT.Exp,
                                                         bias=KM[:, v, 2 * j + h:2 * j + h + 1],
                                                         accum_out=KS[:, v, 2 * j + h:2 * j + h + 1])
                            a.then_inc(emptied[k], 1)
                        if tail and j == 0:
                            k = U.bank((key, "ctx"))
                            act.wait_ge(filled[k], U.done((key, "ctx"), i))
                            c = bank[k][:, :].rearrange("p (j n) -> p j n", n=P)
                            nc.scalar.activation(CT[0:DH, u, :, 0:DH], c[0:DH, :, 0:DH], ACT.Copy)
                            nc.scalar.activation(CT[DH:P, u, :, DH:P], c[DH:P, :, DH:P], ACT.Copy).then_inc(emptied[k], 1)
                    if proj:
                        copy_out("v0", VV[:, v, 0, :])
                    if norm:
                        modulate(1, key, U, i, b - 1, v)
                    if proj:
                        copy_out("v1", VV[:, v, 1, :])

                act.wait_ge(s_ct0, 1)
                run_batches(act, batch)
            if phases >= 4:
                def high4(e, u, loads):
                    act.wait_ge(s_we[u], loads)
                    nc.scalar.activation(WEH[:, u, :], WE[:, u, 0:FT * P], ACT.Copy).then_inc(s_we_hi, 1)

                def expert4(e, u, loads, at_least):
                    for g in range(NG):
                        k = g % 2
                        for f in range(FT):
                            act.wait_ge(filled[f], 4 * e + (base4[f] + g + 1))
                            if f == 0 and not (at_least == 0 and g < 2):
                                act.wait_ge(filled[4 + k], 2 * e + (base4[4 + k] + g // 2))
                            nc.scalar.activation(HF[:, k, f, :], bank[f][:, :], ACT.Relu,
                                                 bias=WE[:, u, 2 * FT * P + f:2 * FT * P + f + 1]).then_inc(emptied[f], 1)
                        if at_least == 0 and g == 0:
                            modulate(1, 8, U_p3[8], 0, 7, 1)
                        if at_least == 0 and g == 1:
                            act.wait_ge(s_logits, 1)
                            nc.scalar.activation(SCO[:, :, 0:E1], SCO[:, :, 0:E1], ACT.Exp).then_inc(s_rexp, 1)
                        if g == 2 and at_least < E1 - 1:
                            high4(e + 1, 1 - u, loads)

                high4(0, 0, 16)
                expert4(0, 0, 16, 0)
                with act.Fori(0, E1 // 2 - 1) as i:
                    expert4(2 * i + 1, 1, 16 * i + 32, 1)
                    expert4(2 * i + 2, 0, 16 * i + 32, 1)
                expert4(E1 - 1, 1, 0, E1 - 1)

        @block.vector
        def _(dve):
            def statistics(k, g):
                for t in range(GT * g, GT * g + GT):
                    a = nc.vector.bn_stats(out=ST[:, t, :], in_=X[:, t, :])
                link(dve, a)
                for t in range(GT * g, GT * g + GT):
                    a = nc.vector.bn_aggr(out=MV[:, t, :], in_=ST[:, t, :])
                a.then_inc(s_var, 1)

            def normed(k, g):
                dve.wait_ge(s_rstd, BEFORE[k] + g + 1)
                if g >= 2:
                    tr = U_b[k].bank(("tr", g - 2))
                    dve.wait_ge(filled[tr], U_b[k].done(("tr", g - 2)))
                for t in range(GT * g, GT * g + GT):
                    a = nc.vector.tensor_scalar(XH[:, g % 2, t - GT * g, :], X[:, t, :], MV[:, t, 0:1], RS[:, t:t + 1],
                                                ALU.subtract, ALU.mult)
                a.then_inc(s_xh, 1)

            def combine(g, gated, count):
                dve.wait_ge(s_gated, gated)
                v = X[:, GT * g:GT * g + GT, :]
                nc.vector.tensor_tensor(v, v, ACC[:, GT * g:GT * g + GT, :], ALU.add).then_inc(x_done, 1)
                dve.wait_ge(x_done, count)

            def boundary(k, before, take=None, between=None):
                U = U_b[k]
                before(0)
                statistics(k, 0)
                for g in range(NG + 2):
                    if g + 1 < NG:
                        before(g + 1)
                        statistics(k, g + 1)
                    if g < NG:
                        normed(k, g)
                    if g == 0 and between is not None:
                        between()
                    if k == 0 and 1 <= g <= NG:
                        q = g - 1
                        tr = U.bank(("tr", q))
                        dve.wait_ge(emptied[tr], U.done(("tr", q)))
                        nc.vector.tensor_tensor(HT[:, 1, GW * q:GW * q + GW], H32[:, q % 2, :],
                                                HT[:, 0, GW * q:GW * q + GW].bitcast(F32), ALU.subtract).then_inc(s_ht, 1)
                    if take is not None and g >= 2:
                        q = g - 2
                        rt = U.bank(("rt", q))
                        dve.wait_ge(filled[rt], U.done(("rt", q)))
                        take(slice(GT * q, GT * q + GT), bank[rt]).then_inc(emptied[rt], 1)
                if take is not None:
                    for q in (NG - 2, NG - 1):
                        dve.wait_ge(emptied[U.bank(("rt", q))], U.done(("rt", q)))

            def take_modulation():
                dve.wait_ge(filled[0], U_mod.done("modT"))
                link(dve, nc.vector.tensor_copy(MODT[:, :, :, :].rearrange("p l q b -> p (l q b)"), bank[0][:, 0:8 * B]))
                v = MODT[:, :, :, :].rearrange("p l (a q) b -> p (l a) q b", q=2)[:, :, 1, :]
                nc.vector.tensor_scalar_add(v, v, 1.0).then_inc(emptied[0], 1)

            def take_decay(tiles, b_):
                b0 = tiles.start // TT
                return nc.vector.tensor_tensor(Z[:, :, b0:b0 + GT // TT, :].rearrange("p c b h -> p b c h"),
                                               b_[:, 0:GT * H0].rearrange("p (b c h) -> p b c h", c=TT, h=H0),
                                               misc_of("bd").unsqueeze(1).unsqueeze(1).to_broadcast([P, GT // TT, TT, H0]),
                                               ALU.add)
            boundary(0, lambda g: dve.wait_ge(s_x[g], 16), take_decay, take_modulation)
            z = Z[:, :, :, :].rearrange("p c b h -> p (c b h)")
            za = ZA[:, :, :, :].rearrange("p c b h -> p (c b h)")
            nc.vector.scalar_tensor_tensor(za, z, -1.0, z, ALU.mult, ALU.min).then_inc(s_nabs, 1)

            def wa_low(c):
                dve.wait_ge(s_wa_hi, c + 1)
                nc.vector.tensor_tensor(WAL[:, c, :], WRAW[c], WAH[:, c, :].bitcast(F32), ALU.subtract).then_inc(s_wa_lo_v, 1)
            wa_low(2)
            wa_low(3)
            dve.wait_ge(s_log, 1)
            nc.vector.scalar_tensor_tensor(z, z, 0.0, za, ALU.max, ALU.add).then_inc(s_ld, 1)
            wa_low(4)
            dve.wait_ge(filled[4], U_n.done("n"))
            link(dve, nc.vector.tensor_copy(N_HI.bitcast(F32R), bank[4][:, 0:S]))
            nc.vector.tensor_tensor(N_LO.bitcast(F32R), bank[4][:, 0:S], N_HI, ALU.subtract).then_inc(emptied[4], 1)
            dve.wait_ge(s_wo, 32)
            nc.vector.tensor_tensor(WOR[:, :, :], WOR[:, :, :], misc_of("norm_w").unsqueeze(2).to_broadcast([P, HT0, D]),
                                    ALU.mult).then_inc(s_wo_n, 1)
            if phases >= 1:
                def projections(key, U, i, hh, names):
                    for name in names:
                        j, k = int(name[1]), U.bank((key, name)) if name[0] in "kv" else None
                        if name[0] == "k":
                            g = U.bank((key, f"g{j}"))
                            dve.wait_ge(emptied[g], U.done((key, f"g{j}"), i))
                            dve.wait_ge(filled[k], U.done((key, name), i))
                            nc.vector.scalar_tensor_tensor(
                                KG[:, hh, 2 * j:2 * j + 2, :].rearrange("p m t -> p (m t)"), TG[:, j, :], 1.0,
                                bank[k][:, :], ALU.add, ALU.mult).then_inc(emptied[k], 1)
                        elif name[0] == "v":
                            dve.wait_ge(filled[k], U.done((key, name), i))
                            nc.vector.tensor_copy(V[:, hh, j, :], bank[k][:, :]).then_inc(emptied[k], 1)

                def weigh(n, hh, p):
                    m, par = 3 * n + p, (hh + p) % 2
                    dve.wait_ge(mask_done, 2 * m + 2)
                    if p == 0:
                        dve.wait_ge(av_done, 2 * n)
                    elif p == 1:
                        dve.wait_ge(filled[5], n + base1[5])
                    else:
                        dve.wait_ge(av_done, 2 * n + 1)
                    for e in range(2):
                        dve.wait_ge(filled[2 + e], m + (base1[2 + e] + 1))
                        nc.vector.tensor_tensor(PB[:, par, e, :], bank[2 + e][:, :], DB[:, par, e, :],
                                                ALU.mult).then_inc(emptied[2 + e], 1)

                def gate_outputs(n, hh):
                    dve.wait_ge(sq_done, 2 * n + 2)
                    for k in range(2):
                        nc.vector.scalar_tensor_tensor(
                            OT[:, hh, 2 * k:2 * k + 2, :].rearrange("p m t -> p (m t)"),
                            TO[:, hh, 2 * k:2 * k + 2, :].rearrange("p m t -> p (m t)"), 1.0, bank[4 + k][:, :],
                            ALU.add, ALU.mult).then_inc(emptied[4 + k], 1)

                def add_attention(key, U, i, b, u):
                    dve.wait_ge(s_gb, 16)
                    dve.wait_ge(s_rms, b + 1)
                    k = U.bank((key, "y"))
                    dve.wait_ge(filled[k], U.done((key, "y"), i))
                    for t in range(TT):
                        a = nc.vector.scalar_tensor_tensor(TMP[:, t:t + 1, :], bank[k][:, D * t:D * t + D].unsqueeze(1),
                                                           SR[:, u, t:t + 1], GB[:, 0, bass.ds(b, 1), :],
                                                           ALU.mult, ALU.mult)
                    a.then_inc(emptied[k], 1)
                    dve.wait_ge(emptied[k], U.done((key, "y"), i))
                    v = X[:, bass.ds(TT * b, TT), :]
                    nc.vector.tensor_tensor(v, v, TMP[:, :, :], ALU.add).then_inc(x_done, 1)

                def carry():
                    nc.vector.memset(PAD[:, :], 0.0)

                def batch_statistics(k, c, v):
                    dve.wait_ge(x_done, c + ((0, 1, 0, B + NG + 1)[k]))
                    carry()
                    for t in range(TT):
                        a = nc.vector.bn_stats(out=BST[:, v, t:t + 1, :], in_=X[:, bass.ds(TT * c + t, 1), :])
                    link(dve, a)
                    carry()
                    for t in range(TT):
                        a = nc.vector.bn_aggr(out=BMV[:, v, t, :], in_=BST[:, v, t, :])
                    a.then_inc(s_var, 1)

                def batch_normed(k, c, v):
                    dve.wait_ge(s_rstd, c + (BEFORE[k] + 1))
                    for t in range(TT):
                        a = nc.vector.tensor_scalar(XH[:, v, t:t + 1, :], X[:, bass.ds(TT * c + t, 1), :], BMV[:, v, t, 0:1],
                                                    BRS[:, v, t:t + 1], ALU.subtract, ALU.mult)
                    a.then_inc(s_xh, 1)

                def batch_low(key, U, i, c, v):
                    k = U.bank((key, "tr"))
                    dve.wait_ge(emptied[k], U.done((key, "tr"), i))
                    h = bass.ds(S * c, S)
                    nc.vector.tensor_tensor(HT[:, 1, h], H32[:, v, 0:S], HT[:, 0, h].bitcast(F32), ALU.subtract).then_inc(s_ht, 1)

                def batch_route(key, U, i, c, v):
                    k = U.bank((key, "rt"))
                    dve.wait_ge(emptied[k], U.done((key, "rt"), i))
                    left, score, choice = LEFT[:, v, :, :], SCORE[:, v, :, :], CHOICE[:, v, :, :]
                    link(dve, nc.vector.tensor_scalar_add(left, left, 1.0))
                    link(dve, nc.vector.reciprocal(score, left))
                    link(dve, nc.vector.tensor_tensor(choice, score, misc_of("ebias").unsqueeze(1).to_broadcast([P, TT, E0]),
                                                      ALU.add))
                    carry()
                    for t in range(TT):
                        a = nc.vector.max(out=TOP8[:, v, t, :], in_=choice[:, t, :])
                    link(dve, a)
                    carry()
                    for t in range(TT):
                        a = nc.vector.match_replace(out=left[:, t, :], in_to_replace=TOP8[:, v, t, :],
                                                    in_values=choice[:, t, :], imm_value=-BIG)
                    link(dve, a)
                    link(dve, nc.vector.tensor_tensor(left, left, choice, ALU.not_equal))
                    link(dve, nc.vector.tensor_tensor(left, left, score, ALU.mult))
                    link(dve, nc.vector.tensor_reduce(out=TOTAL[:, v, :], in_=left, axis=AX_X, op=ALU.add))
                    link(dve, nc.vector.reciprocal(TOTAL[:, v, :], TOTAL[:, v, :]))
                    link(dve, nc.vector.tensor_scalar(TOTAL[:, v, :], TOTAL[:, v, :], ROUTE_SCALE, None, ALU.mult))
                    nc.vector.tensor_tensor(COMB[:, bass.ds(TT * c, TT), 1:E0 + 1], left,
                                            TOTAL[:, v, :].unsqueeze(2).to_broadcast([P, TT, E0]), ALU.mult).then_inc(s_comb, 1)

                def half(key, U, i, n, b, hh, u, at_least):
                    norm = hh == 1 and at_least >= 2
                    for p in range(3):
                        weigh(n, hh, p)
                        if norm and p == 0:
                            batch_statistics(1, b - 1, 1 - u)
                        if p == 0 and at_least >= 1:
                            gate_outputs(n - 1, 1 - hh)
                        if p == 2 and hh == 0 and at_least >= 2:
                            add_attention(key, U, i, b - 1, 1 - u)
                        if at_least < 15:
                            projections(key, U, i, 1 - hh, PROJ[p])
                        if norm and p == 0:
                            batch_normed(1, b - 1, 1 - u)
                        if norm and p == 1:
                            batch_low(key, U, i, b - 1, 1 - u)
                        if norm and p == 2:
                            batch_route(key, U, i, b - 1, 1 - u)

                for names in PROJ:
                    projections(-1, U_p1[-1], 0, 0, names)
                dve.wait_ge(filled[5], U_mod.done("gates"))
                gates = bank[5][0:B, :]
                ga = GA[:, :, :].rearrange("b k d -> b (k d)")
                gs = GS[:, :, :].rearrange("b k d -> b (k d)")
                nc.vector.tensor_scalar(gs, gates, 0.0, 2.0, ALU.is_ge, ALU.mult)
                link(dve, nc.vector.tensor_scalar(ga, gates, 0.25, None, ALU.max))
                nc.vector.scalar_tensor_tensor(ga, gates, -1.0, ga, ALU.mult, ALU.max).then_inc(emptied[5], 1)
                dve.wait_ge(emptied[5], U_mod.done("gates"))
                nc.vector.scalar_tensor_tensor(gs, gs, 1.0, ga, ALU.subtract, ALU.mult).then_inc(s_gates, 1)
                dve.wait_ge(s_nout, 32)
                run_halves(dve, half)
                gate_outputs(15, 1)
                add_attention(16, U_p1[16], 0, 7, 1)

                nc.vector.memset(COMB[:, :, 0:1], 1.0)
                batch_statistics(1, 7, 1)
                batch_normed(1, 7, 1)
                batch_low(16, U_p1[16], 0, 7, 1)
                batch_route(16, U_p1[16], 0, 7, 1)
            if phases >= 2:
                dve.wait_ge(s_comb, B)

                def first_expert(g):
                    k = 4 + g % 2
                    dve.wait_ge(filled[k], base2[k] + g // 2 + 1)
                    nc.vector.tensor_copy(ACC[:, GT * g:GT * g + GT, :].rearrange("p t d -> p (t d)"),
                                          bank[k][:, :]).then_inc(emptied[k], 1)

                def add_expert(x, g, y_base, at_least):
                    k = 4 + g % 2
                    dve.wait_ge(filled[k], 2 * x + (y_base[k] + g // 2 + 1))
                    if at_least:
                        dve.wait_ge(emptied[k], 2 * x + (y_base[k] + g // 2 - 1))
                    for t in range(GT):
                        v = ACC[:, GT * g + t, :]
                        a = nc.vector.scalar_tensor_tensor(v, bank[k][:, D * t:D * t + D],
                                                           COMB[:, GT * g + t, bass.ds(x, 1)], v, ALU.mult, ALU.add)
                    a.then_inc(emptied[k], 1)

                def hidden(x, g, at_least):
                    k = g % 2
                    dve.wait_ge(emptied[k], 2 * x + (base2[k] + g // 2 + 1))
                    dve.wait_ge(filled[2 + k], 2 * x + (base2[2 + k] + g // 2 + 1))
                    if at_least or g >= 2:
                        dve.wait_ge(filled[4 + k], 2 * x + (base2[4 + k] + g // 2))
                    nc.vector.tensor_tensor(HB[:, k, :], SIL[:, k, :], bank[2 + k][:, :], ALU.mult).then_inc(emptied[2 + k], 1)

                def expert(x, at_least):
                    for g in range(NG):
                        hidden(x, g, at_least)
                        if g == 0 and at_least == 0:
                            continue
                        if at_least == 0 or (at_least == 1 and g == 0):
                            first_expert((g - 1) % NG)
                        elif g:
                            add_expert(x, g - 1, base2, at_least)
                        else:
                            add_expert(x - 1, NG - 1, base2, at_least - 1)

                expert(0, 0)
                expert(1, 1)
                with dve.Fori(0, (E0 - 2) // 2) as i:
                    expert(2 * i + 2, 2)
                    expert(2 * i + 3, 2)
                expert(E0, 2)
                add_expert(E0, NG - 1, base2, 1)
                boundary(2, lambda g: combine(g, g + 1, B + g + 1))
            if phases >= 3:
                def q_scores(key, U, i, v, t):
                    k = U.bank((key, f"q{t}"))
                    dve.wait_ge(filled[k], U.done((key, f"q{t}"), i))
                    q = bank[k][:, :].rearrange("p (h d) -> p h d", d=DH)
                    link(dve, nc.vector.tensor_reduce(out=QM[:, v, t, :], in_=q, axis=AX_X, op=ALU.max))
                    nc.vector.tensor_tensor(QE[:, v, t, :].rearrange("p (h d) -> p h d", d=DH), q,
                                            QM[:, v, t, :].unsqueeze(2).to_broadcast([P, H1, DH]),
                                            ALU.subtract).then_inc(emptied[k], 1)

                def q_sums(b, v, t):
                    dve.wait_ge(s_qe, 2 * b + (t + 1))
                    e = QE[:, v, t, :].rearrange("p (h d) -> p h d", d=DH)
                    link(dve, nc.vector.tensor_reduce(out=QS[:, v, t, :], in_=e, axis=AX_X, op=ALU.add))
                    nc.vector.reciprocal(QS[:, v, t, :], QS[:, v, t, :]).then_inc(s_qs, 1)

                def take_logits(key, U, i, c):
                    k = U.bank((key, "rt"))
                    dve.wait_ge(filled[k], U.done((key, "rt"), i))
                    nc.vector.tensor_tensor(VAL[:, bass.ds(TT * c, TT), 0:E1],
                                            bank[k][:, 0:TT * E1].rearrange("p (t e) -> p t e", e=E1),
                                            misc_of("b_router").unsqueeze(1).to_broadcast([P, TT, E1]),
                                            ALU.add).then_inc(emptied[k], 1)

                def batch(key, U, i, b, u, tail, proj, norm):
                    v = 1 - u
                    if proj:
                        for t in range(TT):
                            q_scores(key, U, i, v, t)
                    if norm:
                        batch_statistics(3, b - 1, v)
                    if proj:
                        for j in range(2):
                            k = U.bank((key, f"k{j}"))
                            dve.wait_ge(filled[k], U.done((key, f"k{j}"), i))
                            link(dve, nc.vector.tensor_reduce(out=KM[:, v, 2 * j:2 * j + 2],
                                                              in_=bank[k][:, :].rearrange("p (j t) -> p j t", t=S),
                                                              axis=AX_X, op=ALU.max))
                            nc.vector.tensor_scalar(KM[:, v, 2 * j:2 * j + 2], KM[:, v, 2 * j:2 * j + 2], -1.0, None,
                                                    ALU.mult).then_inc(s_kmax, 1)
                    if norm:
                        batch_normed(3, b - 1, v)
                    if tail:
                        link(dve, nc.vector.reciprocal(RK[:, u, :], KS[:, u, :]))
                        link(dve, nc.vector.tensor_scalar(RK[:, u, :], RK[:, u, :], DH ** -0.5, None, ALU.mult))
                    if proj:
                        q_sums(b + 1, v, 0)
                    if tail:
                        k = U.bank((key, "m"))
                        dve.wait_ge(filled[k], U.done((key, "m"), i))
                        nc.vector.tensor_tensor(MS[:, u, :, :], bank[k][:, :].rearrange("p (j n) -> p j n", n=D),
                                                RK[:, u, :].unsqueeze(2).to_broadcast([P, HT1, D]),
                                                ALU.mult).then_inc(emptied[k], 1)
                    if proj:
                        q_sums(b + 1, v, 1)
                    if norm:
                        batch_low(key, U, i, b - 1, v)
                        take_logits(key, U, i, b - 1)
                    if tail:
                        k = U.bank((key, "y"))
                        dve.wait_ge(filled[k], U.done((key, "y"), i))
                        nc.vector.tensor_tensor(YT[:, u, :, :], bank[k][:, 0:TT * D].rearrange("p (t d) -> p t d", d=D),
                                                misc_of("bo").unsqueeze(1).to_broadcast([P, TT, D]),
                                                ALU.add).then_inc(emptied[k], 1)
                        dve.wait_ge(emptied[k], U.done((key, "y"), i))
                        link(dve, nc.vector.tensor_tensor(YT[:, u, :, :], YT[:, u, :, :],
                                                          GB[:, 0, bass.ds(b, 1), :].to_broadcast([P, TT, D]), ALU.mult))
                        x_ = X[:, bass.ds(TT * b, TT), :]
                        nc.vector.tensor_tensor(x_, x_, YT[:, u, :, :], ALU.add).then_inc(x_done, 1)

                dve.wait_ge(s_gb, 32)
                nc.vector.memset(VAL[:, :, E1:E1 + 6], BIG)
                run_batches(dve, batch)
                batch_statistics(3, 7, 1)
                batch_normed(3, 7, 1)
                batch_low(8, U_p3[8], 0, 7, 1)
                take_logits(8, U_p3[8], 0, 7)
                dve.wait_ge(emptied[U_p3[8].bank((8, "rt"))], U_p3[8].done((8, "rt")))
                for t in range(NT):
                    a = nc.vector.max(out=M8[:, t, :], in_=VAL[:, t, :])
                link(dve, a)
                nc.vector.tensor_tensor(SCO[:, :, 0:E1], VAL[:, :, 0:E1], M8[:, :, 6:7].to_broadcast([P, NT, E1]),
                                        ALU.subtract).then_inc(s_logits, 1)
                for t in range(NT):
                    a = nc.vector.match_replace(out=REP[:, t, 0:E1 + 6], in_to_replace=M8[:, t, :], in_values=VAL[:, t, :],
                                                imm_value=-BIG)
                link(dve, a)
                link(dve, nc.vector.tensor_tensor(SEL[:, :, 0:E1], REP[:, :, 0:E1], VAL[:, :, 0:E1], ALU.not_equal))
                dve.wait_ge(s_rexp, 1)
                link(dve, nc.vector.tensor_tensor(SEL[:, :, 0:E1], SEL[:, :, 0:E1], SCO[:, :, 0:E1], ALU.mult))
                link(dve, nc.vector.tensor_reduce(out=SUM[:, :], in_=SEL[:, :, 0:E1], axis=AX_X, op=ALU.add))
                link(dve, nc.vector.reciprocal(SUM[:, :], SUM[:, :]))
                nc.vector.tensor_tensor(COMB[:, :, 0:E1], SEL[:, :, 0:E1], SUM[:, :].unsqueeze(2).to_broadcast([P, NT, E1]),
                                        ALU.mult).then_inc(s_comb, 1)
            if phases >= 4:
                for g in range(NG):
                    k = U_wt.bank(("wt", g))
                    dve.wait_ge(filled[k], U_wt.done(("wt", g)))
                    nc.vector.tensor_copy(WT[:, GW * g:GW * g + GW], bank[k][0:E1, :]).then_inc(emptied[k], 1)
                for g in range(NG):
                    k = U_wt.bank(("b2", g))
                    dve.wait_ge(filled[k], U_wt.done(("b2", g)))
                    nc.vector.tensor_copy(ACC[:, GT * g:GT * g + GT, :].rearrange("p t d -> p (t d)"),
                                          bank[k][:, :]).then_inc(emptied[k], 1)
                for g in (NG - 2, NG - 1):
                    dve.wait_ge(emptied[U_wt.bank(("b2", g))], U_wt.done(("b2", g)))

                def expert4(e, at_least):
                    for g in range(NG):
                        if g:
                            add_expert(e, g - 1, base4, at_least)
                        elif at_least:
                            add_expert(e - 1, NG - 1, base4, at_least - 1)
                expert4(0, 0)
                expert4(1, 1)
                with dve.Fori(0, (E1 - 2) // 2) as i:
                    expert4(2 * i + 2, 2)
                    expert4(2 * i + 3, 2)
                add_expert(E1 - 1, NG - 1, base4, 1)
                for g in range(NG):
                    combine(g, NG + g + 1, 2 * B + NG + g + 1)

        @block.tensor
        def _(pe):
            def mm(out_, lhsT, rhs, start, stop, **kw):
                return nc.tensor.matmul(out_, lhsT, rhs, start=start, stop=stop, **kw)

            def open_bank(U, name, i=0):
                k = U.bank(name)
                pe.wait_ge(emptied[k], U.free(name, i))
                return k

            def split_product(out_, lhsT, rhs):
                for n, (a, b_) in enumerate(((0, 0), (0, 1), (1, 0))):
                    last = mm(out_, lhsT(a), rhs(b_), n == 0, n == 2)
                return last

            pe.wait_ge(s_silu, 1)
            pe.wait_ge(s_mod, 16)
            for l in range(2):
                for q, part in enumerate((0, 1, 3, 4)):
                    a = mm(bank[0][:, (4 * l + q) * B:(4 * l + q + 1) * B], WM[:, l, part * D:part * D + D], SC[:, l, :],
                           True, True)
            a.then_inc(filled[0], 1)
            def boundary(k, weights, width):
                U = U_b[k]
                for g in range(NG + 1):
                    if g < NG:
                        pe.wait_ge(s_xh, BEFORE[k] + g + 1)
                        b_ = open_bank(U, ("tr", g))
                        for t in range(GT):
                            a = nc.tensor.transpose(bank[b_][:, P * t:P * t + P], XH[:, g % 2, t, :], IDN[:, :])
                        a.then_inc(filled[b_], 1)
                    if g and weights is not None:
                        q = g - 1
                        tr = U.bank(("tr", q))
                        pe.wait_ge(emptied[tr], U.done(("tr", q)))
                        b_ = open_bank(U, ("rt", q))
                        for t in range(GT):
                            a = mm(bank[b_][:, width * t:width * t + width], H32[:, q % 2, P * t:P * t + P], weights,
                                   True, True)
                        a.then_inc(filled[b_], 1)

            pe.wait_ge(s_idn, 2)
            pe.wait_ge(s_misc, 16)
            boundary(0, misc_of("wd"), H0)
            for l in range(2):
                for q, part in enumerate((2, 5)):
                    a = mm(bank[5][0:B, (2 * l + q) * D:(2 * l + q + 1) * D], SC[:, l, :], WM[:, l, part * D:part * D + D],
                           True, True)
            a.then_inc(filled[5], 1)

            pe.wait_ge(s_ld, 1)
            pe.wait_ge(s_tri, 2)
            b_ = open_bank(U_n, "n")
            for t in range(TT):
                for c in range(t + 1):
                    a = mm(bank[b_][:, P * t:P * t + P], Z[:, c, :, :].rearrange("p b h -> p (b h)"), TRI[:, P * (t - c):P * (t - c) + P], c == 0, c == t)
            a.then_inc(filled[b_], 1)

            if phases >= 1:
                def projections(key, U, i, hh, u, names):
                    for name in names:
                        what, j = "qkvgo".index(name[0]), int(name[1])
                        k = open_bank(U, (key, name), i)
                        w = (WAH, WAL)
                        if name[0] != "v":
                            for m in range(2):
                                c = (4 * hh + 2 * j + m) * P
                                a = split_product(bank[k][:, S * m:S * m + S], lambda p_: w[p_][:, what, c:c + P],
                                                  lambda p_: HTB[:, u, p_, :])
                        else:
                            c = hh * HALF * DH
                            a = split_product(bank[k][:, :], lambda p_: HTB[:, u, p_, P * j:P * j + P],
                                              lambda p_: w[p_][:, what, c:c + HALF * DH])
                        a.then_inc(filled[k], 1)

                def arguments(m, kind, hh, u, lg_loads, rg_loads):
                    pe.wait_ge(s_lg[u], lg_loads)
                    pe.wait_ge(s_rg[hh], rg_loads)
                    v = RG[:, hh, :, :].rearrange("k (h two) t -> k two h t", two=2)
                    for e in range(2):
                        pe.wait_ge(emptied[e], m + base1[e])
                        if kind < 2:
                            a = mm(bank[e][:, :], LG[:, u, 0:P], v[:, e, 2 * kind:2 * kind + 2, :], True, True)
                        else:
                            a = mm(bank[e][:, :], LG[:, u, P:S], v[:, e, :, P:S], True, True)
                        a.then_inc(filled[e], 1)

                def scores(m, kind, hh):
                    for e in range(2):
                        pe.wait_ge(emptied[2 + e], m + base1[2 + e])
                    steps = 2 if kind < 2 else 4
                    for n in range(steps):
                        for e in range(2):
                            r = slice(DH * e, DH * e + DH)
                            if kind < 2:
                                j = 2 * kind + n
                                a = mm(bank[2 + e][:, S * n:S * n + S], KG[r, hh, j, 0:P], Q[r, hh, j, :], True, True)
                            else:
                                a = mm(bank[2 + e][:, P * n:P * n + P], KG[r, hh, n, P:S], Q[r, hh, n, P:S], True, True)
                            if n == steps - 1:
                                a.then_inc(filled[2 + e], 1)

                def outputs(n, m, kind, hh, par):
                    for e in range(2):
                        pe.wait_ge(emptied[2 + e], m + (base1[2 + e] + 1))
                    if kind < 2:
                        pe.wait_ge(emptied[4 + kind], n + base1[4 + kind])
                        for x_ in range(2):
                            h = 4 * kind + 2 * x_
                            for e in range(2):
                                a = mm(bank[4 + kind][DH * e:DH * e + DH, S * x_:S * x_ + S],
                                       V[:, hh, 0, DH * (h + e):DH * (h + e) + DH], PB[:, par, e, S * x_:S * x_ + S],
                                       x_ == 0, True, skip_group_check=True)
                        a.then_inc(av_done, 1)
                    else:
                        for x_ in range(4):
                            c = S * (x_ % 2) + P
                            for e in range(2):
                                h = 2 * x_ + e
                                a = mm(bank[4 + x_ // 2][DH * e:DH * e + DH, c:c + P],
                                       V[:, hh, 1, DH * h:DH * h + DH], PB[:, par, e, P * x_:P * x_ + P],
                                       False, True, skip_group_check=True)
                            if x_ % 2:
                                a.then_inc(filled[4 + x_ // 2], 1)

                def token_squares(key, U, i, b):
                    pe.wait_ge(s_ssq, b + 1)
                    k = open_bank(U, (key, "ss"), i)
                    for t in range(TT):
                        a = mm(bank[k][:, t:t + 1], SSQ[:, P * t:P * t + P], ONE[:, :], True, True)
                    a.then_inc(filled[k], 1)

                def output_projection(key, U, i):
                    k = open_bank(U, (key, "y"), i)
                    for t in range(TT):
                        for j in range(HT0):
                            a = mm(bank[k][:, D * t:D * t + D], OT[:, j // 4, j % 4, P * t:P * t + P], WOR[:, j, :],
                                   j == 0, j == HT0 - 1)
                    a.then_inc(filled[k], 1)

                def turn_normed(k_, key, U, i, c, v):
                    pe.wait_ge(s_xh, c + (BEFORE[k_] + 1))
                    k = open_bank(U, (key, "tr"), i)
                    for t in range(TT):
                        a = nc.tensor.transpose(bank[k][:, P * t:P * t + P], XH[:, v, t, :], IDN[:, :])
                    a.then_inc(filled[k], 1)

                def route(key, U, i, v, weights, width):
                    k = U.bank((key, "tr"))
                    if k != U.bank((key, "rt")):
                        pe.wait_ge(emptied[k], U.done((key, "tr"), i))
                    k = open_bank(U, (key, "rt"), i)
                    for t in range(TT):
                        a = mm(bank[k][:, width * t:width * t + width], H32[:, v, P * t:P * t + P], weights, True, True)
                    a.then_inc(filled[k], 1)

                def half(key, U, i, n, b, hh, u, at_least):
                    norm = hh == 1 and at_least >= 2
                    for k in (6, 7):
                        pe.wait_ge(emptied[k], U.before(key, k, i))
                    if at_least == 2:
                        loads = {0: i + 1, 1: i + 1, 2: i + 2, 3: i + 2, 4: i + 2}
                        loads_b, loads_next = loads[key], loads[key + 1]
                    else:
                        loads_b, loads_next = b // 2 + 1, (b + hh) // 2 + 1
                    b_next, u_next = b + hh, (u + hh) % 2
                    for p in range(3):
                        scores(3 * n + p, p, hh)
                        if p < 2:
                            arguments(3 * n + (p + 1), p + 1, hh, u, 32 * loads_b, 16 * (b + 1))
                        elif at_least < 15:
                            arguments(3 * n + 3, 0, 1 - hh, u_next, 32 * loads_next, 16 * (b_next + 1))
                        if p == 1 and hh == 0 and at_least >= 2:
                            token_squares(key, U, i, b - 1)
                        if p == 2 and hh == 0 and at_least >= 2:
                            output_projection(key, U, i)
                        if at_least < 15:
                            if p == 0:
                                pe.wait_ge(s_htb[u_next], 16 * loads_next)
                            projections(key, U, i, 1 - hh, u_next, PROJ[p])
                        if norm and p == 1:
                            turn_normed(1, key, U, i, b - 1, 1 - u)
                        if norm and p == 2:
                            route(key, U, i, 1 - u, misc_of("gate_w"), E0)
                        outputs(n, 3 * n + p, p, hh, (hh + p) % 2)

                pe.wait_ge(s_wa_hi, 5)
                pe.wait_ge(s_wa_lo, 2)
                pe.wait_ge(s_wa_lo_v, 3)
                pe.wait_ge(s_htb[0], 16)
                for names in PROJ:
                    projections(-1, U_p1[-1], 0, 0, 0, names)
                arguments(0, 0, 0, 0, 32, 16)
                pe.wait_ge(s_wo_n, 1)
                run_halves(pe, half)
                for k in range(2):
                    pe.wait_ge(emptied[4 + k], HALVES + base1[4 + k])
                output_projection(16, U_p1[16], 0)
                token_squares(16, U_p1[16], 0, 7)
            if phases >= 2:
                def expert_products(x, u, g):
                    k = g % 2
                    for q in range(2):
                        pe.wait_ge(emptied[2 * q + k], 2 * x + (base2[2 * q + k] + g // 2))
                        w = (FWH, FWL)
                        split_product(bank[2 * q + k][:, :], lambda p_: w[p_][:, u, P * q:P * q + P],
                                      lambda p_: HT[:, p_, GW * g:GW * g + GW]).then_inc(filled[2 * q + k], 1)

                def expert_down(x, u, g):
                    k = g % 2
                    pe.wait_ge(emptied[2 + k], 2 * x + (base2[2 + k] + g // 2 + 1))
                    pe.wait_ge(emptied[4 + k], 2 * x + (base2[4 + k] + g // 2))
                    for t in range(GT):
                        a = mm(bank[4 + k][:, D * t:D * t + D], HB[:, k, P * t:P * t + P], FW[:, u, 2, :], True, True)
                    a.then_inc(filled[4 + k], 1)

                def expert(x, u, at_least):
                    pe.wait_ge(s_fw_hi, x + 1)
                    pe.wait_ge(s_fw_lo, x + 1)
                    for g in range(NG):
                        expert_products(x, u, g)
                        if g:
                            expert_down(x, u, g - 1)
                        elif at_least:
                            expert_down(x - 1, 1 - u, NG - 1)
                pe.wait_ge(s_fw_hi, 1)
                pe.wait_ge(s_fw_lo, 1)
                pe.wait_ge(s_ht, BEFORE[2] - 1)
                expert_products(0, 0, 0)
                expert_products(0, 0, 1)
                turn_normed(1, 16, U_p1[16], 0, 7, 1)
                route(16, U_p1[16], 0, 1, misc_of("gate_w"), E0)
                expert_down(0, 0, 0)
                expert_products(0, 0, 2)
                expert_down(0, 0, 1)
                pe.wait_ge(s_ht, BEFORE[2])
                expert_products(0, 0, 3)
                expert_down(0, 0, 2)
                with pe.Fori(0, E0 // 2) as i:
                    expert(2 * i + 1, 1, 1)
                    expert(2 * i + 2, 0, 1)
                expert_down(E0, 0, NG - 1)
                boundary(2, None, 0)
            if phases >= 3:
                def project1(key, U, i, v, name):
                    j = int(name[1])
                    k = open_bank(U, (key, name), i)
                    w = (WLH, WLL)
                    if name[0] == "k":
                        for h in range(2):
                            c = P * (2 * j + h)
                            a = split_product(bank[k][:, S * h:S * h + S], lambda p_: w[p_][:, 1, c:c + P],
                                              lambda p_: HTB[:, v, p_, :])
                    else:
                        what = 0 if name[0] == "q" else 2
                        a = split_product(bank[k][:, :], lambda p_: HTB[:, v, p_, P * j:P * j + P],
                                          lambda p_: w[p_][:, what, :])
                    a.then_inc(filled[k], 1)

                def batch(key, U, i, b, u, tail, proj, norm):
                    v = 1 - u
                    if tail:
                        for t in range(TT):
                            open_bank(U, (key, f"kT{t}"), i)
                        for t in range(TT):
                            k = U.bank((key, f"kT{t}"))
                            for j in range(HT1):
                                a = nc.tensor.transpose(bank[k][:, P * j:P * j + P], KE[:, u, j, P * t:P * t + P], IDN[:, :])
                            a.then_inc(filled[k], 1)
                    if proj:
                        loads = {-1: 5, 0: 5, 1: i + 6, 2: i + 6}[key]
                        pe.wait_ge(s_htb[v], 16 * loads)
                        project1(key, U, i, v, "q0")
                        project1(key, U, i, v, "q1")
                    if tail:
                        pe.wait_ge(s_qn, 2 * b + 2)
                        for q in range(2):
                            k = open_bank(U, (key, f"qT{q}"), i)
                            for j in range(2):
                                for t in range(TT):
                                    a = nc.tensor.transpose(bank[k][:, S * j + P * t:S * j + P * t + P],
                                                            QN[:, u, t, P * (2 * q + j):P * (2 * q + j) + P], IDN[:, :])
                            a.then_inc(filled[k], 1)
                    if proj:
                        project1(key, U, i, v, "k0")
                        project1(key, U, i, v, "k1")
                    if tail:
                        for t in range(TT):
                            k = U.bank((key, f"kT{t}"))
                            if k != U.bank((key, "ctx")):
                                pe.wait_ge(emptied[k], U.done((key, f"kT{t}"), i))
                        k = open_bank(U, (key, "ctx"), i)
                        for j in range(HT1):
                            for t in range(TT):
                                a = mm(bank[k][:, P * j:P * j + P], VV[:, u, t, P * j:P * j + P],
                                       KT[:, u, t, P * j:P * j + P], t == 0, t == 1)
                        a.then_inc(filled[k], 1)
                    if proj:
                        project1(key, U, i, v, "v0")
                    if norm:
                        turn_normed(3, key, U, i, b - 1, v)
                    if tail:
                        c = U.bank((key, "ctx"))
                        pe.wait_ge(emptied[c], U.done((key, "ctx"), i))
                        k = open_bank(U, (key, "m"), i)
                        for j in range(HT1):
                            a = mm(bank[k][:, D * j:D * j + D], CT[:, u, j, :], WO1[:, j, :], True, True)
                        a.then_inc(filled[k], 1)
                    if proj:
                        project1(key, U, i, v, "v1")
                    if norm:
                        route(key, U, i, v, misc_of("w_router"), E1)
                    if tail:
                        c = U.bank((key, "m"))
                        pe.wait_ge(emptied[c], U.done((key, "m"), i))
                        pe.wait_ge(emptied[U.bank((key, "qT1"))], U.done((key, "qT1"), i))
                        k = open_bank(U, (key, "y"), i)
                        for t in range(TT):
                            for j in range(HT1):
                                a = mm(bank[k][:, D * t:D * t + D], QT[:, u, j, P * t:P * t + P], MS[:, u, j, :],
                                       j == 0, j == HT1 - 1)
                        a.then_inc(filled[k], 1)

                pe.wait_ge(s_wl_hi, 1)
                pe.wait_ge(s_wl_lo, 1)
                run_batches(pe, batch)
            if phases >= 4:
                def experts_biases():
                    pe.wait_ge(s_comb, B + 1)
                    for g in range(NG):
                        k = open_bank(U_wt, ("wt", g))
                        for t in range(GT):
                            a = mm(bank[k][0:E1, P * t:P * t + P], COMB[:, GT * g + t, 0:E1], IDN[:, :], True, True)
                        a.then_inc(filled[k], 1)
                    for g in range(NG):
                        k = open_bank(U_wt, ("b2", g))
                        for t in range(GT):
                            a = mm(bank[k][:, D * t:D * t + D], WT[:, GW * g + P * t:GW * g + P * t + P], B2[:, :], True, True)
                        a.then_inc(filled[k], 1)

                def expert4_hidden(e, u, g):
                    w = (WEH, WEL)
                    for f in range(FT):
                        pe.wait_ge(emptied[f], 4 * e + (base4[f] + g))
                        split_product(bank[f][:, :], lambda p_: w[p_][:, u, P * f:P * f + P],
                                      lambda p_: HT[:, p_, GW * g:GW * g + GW]).then_inc(filled[f], 1)

                def expert4_down(e, u, g):
                    k = g % 2
                    pe.wait_ge(emptied[FT - 1], 4 * e + (base4[FT - 1] + g + 1))
                    pe.wait_ge(emptied[4 + k], 2 * e + (base4[4 + k] + g // 2))
                    for t in range(GT):
                        for f in range(FT):
                            a = mm(bank[4 + k][:, D * t:D * t + D], HF[:, k, f, P * t:P * t + P],
                                   WE[:, u, P * (FT + f):P * (FT + f) + P], f == 0, f == FT - 1)
                    a.then_inc(filled[4 + k], 1)

                def expert4(e, u, at_least):
                    pe.wait_ge(s_we_hi, e + 1)
                    pe.wait_ge(s_we_lo, e + 1)
                    for g in range(NG):
                        expert4_hidden(e, u, g)
                        if g:
                            expert4_down(e, u, g - 1)
                        elif at_least:
                            expert4_down(e - 1, 1 - u, NG - 1)
                pe.wait_ge(s_we_hi, 1)
                pe.wait_ge(s_we_lo, 1)
                pe.wait_ge(s_ht, BEFORE[3] + B - 1)
                expert4_hidden(0, 0, 0)
                expert4_hidden(0, 0, 1)
                turn_normed(3, 8, U_p3[8], 0, 7, 1)
                expert4_down(0, 0, 0)
                route(8, U_p3[8], 0, 1, misc_of("w_router"), E1)
                expert4_hidden(0, 0, 2)
                experts_biases()
                expert4_down(0, 0, 1)
                pe.wait_ge(s_ht, BEFORE[3] + B)
                expert4_hidden(0, 0, 3)
                expert4_down(0, 0, 2)
                with pe.Fori(0, E1 // 2 - 1) as i:
                    expert4(2 * i + 1, 1, 1)
                    expert4(2 * i + 2, 0, 1)
                expert4(E1 - 1, 1, 1)
                expert4_down(E1 - 1, 1, NG - 1)


def lay_out(i):
    t = np.transpose
    f = np.ascontiguousarray

    def rows(w, n):
        return t(w.reshape(n, P, -1), (1, 0, 2))

    small = {
        "c": np.concatenate([t(i["L0_c"]), t(i["L1_c"])], 1),
        "wd": t(i["L0_attn_Wd"]),
        "bd": np.broadcast_to(i["L0_attn_bd"], (P, H0)),
        "norm_w": t(i["L0_attn_norm_w"].reshape(HT0, P)),
        "gate_w": t(i["L0_ffn_gate_w"]),
        "ebias": np.broadcast_to(i["L0_ffn_expert_bias"], (P, E0)),
        "w_router": i["L1_ffn_W_router"],
        "b_router": np.broadcast_to(i["L1_ffn_b_router"], (P, E1)),
        "bo": np.broadcast_to(i["L1_attn_bo"], (P, D)),
    }
    gate = np.concatenate([i["L0_ffn_shared_gate_w"][None], i["L0_ffn_w_gate"]])
    up = np.concatenate([i["L0_ffn_shared_up_w"][None], i["L0_ffn_w_up"]])
    down = np.concatenate([i["L0_ffn_shared_down_w"][None], i["L0_ffn_w_down"]])
    w2 = i["L1_ffn_W2"].reshape(E1, FT, P, D)
    return {
        "x": f(i["L0_attn_x"]),
        "misc": f(np.concatenate([small[n] for n in MISC], 1)),
        "wmod": f(np.stack([i["L0_wmod"], i["L1_wmod"]], 1)),
        "wa": f(np.stack([t(i["L0_attn_" + n]) for n in ("Wq", "Wk", "Wv", "Wg", "Wog")], 1)),
        "woT": f(rows(t(i["L0_attn_Wo"]), HT0)),
        "w_ffn0": f(np.stack([t(gate, (0, 2, 1)), t(up, (0, 2, 1)), t(down, (0, 2, 1))], 2)),
        "w_l1": f(np.stack([i["L1_attn_" + n] for n in ("Wq", "Wk", "Wv")], 1)),
        "wo1": f(rows(i["L1_attn_Wo"], HT1)),
        "w_ffn1": f(np.concatenate([i["L1_ffn_W1"], t(w2, (0, 2, 1, 3)).reshape(E1, P, FT * D),
                                    t(i["L1_ffn_b1"].reshape(E1, FT, P), (0, 2, 1))], 2)),
        "b2": f(i["L1_ffn_b2"]),
    }


def kernel(**inputs):
    import concourse.bacc as bacc
    from concourse.bass_utils import run_bass_kernel_spmd

    arrays = lay_out({n: np.asarray(a) for n, a in inputs.items()})
    nc = bacc.Bacc("TRN2", target_bir_lowering=False, num_devices=1)
    aps = [nc.dram_tensor(n, a.shape, mybir.dt.from_np(a.dtype), kind="ExternalInput").ap() for n, a in arrays.items()]
    out = nc.dram_tensor("out", (B, S, D), F32, kind="ExternalOutput").ap()
    build(nc, *aps, out)
    r = run_bass_kernel_spmd(nc, [arrays], core_ids=[0])
    return r.results[0]["out"]
```
